# Optimizing a Trainium2 kernel written in Bass

```python
import numpy as np
import jax
import jax.numpy as jnp

def _softmax(x, axis=-1):
    return jax.nn.softmax(x, axis=axis)

def _gelu(x):
    return jax.nn.gelu(x, approximate=True)

def _silu(x):
    return jax.nn.silu(x)

def _sigmoid(x):
    return jax.nn.sigmoid(x)

def _layernorm(x, axis=-1, eps=1e-05):
    m = jnp.mean(x, axis=axis, keepdims=True)
    v = jnp.var(x, axis=axis, keepdims=True)
    return (x - m) / jnp.sqrt(v + eps)

def _scatter_add(tgt, idx, src, axis=0):
    return tgt.at[idx].add(src)

def _segment_sum(src, seg, n):
    return jax.ops.segment_sum(src, seg, n)
kernel_name = 'mk_adaln_d2_jaxref_r8_9ad184'

def setup_inputs(seed: int=0):
    np.random.seed(seed)
    _w = jnp.asarray

    def _L0_attn_setup():
        import jax, jax.numpy as jnp
        import numpy as np
        EPS = 1e-08
        key = jax.random.key(seed)
        x = jax.random.normal(key, (32, 200, 128), dtype=jnp.float32)
        return {'x': x}
    _L0_attn_in = _L0_attn_setup()

    def _L0_ffn_setup():
        import jax, jax.numpy as jnp
        import numpy as np
        D_MODEL = 128
        D_FF = 512
        N_EXPERTS = 8
        TOP_K = 2

        def _ffn(x, w1, b1, w2, b2):
            h = jax.nn.gelu(x @ w1.T + b1)
            return h @ w2.T + b2
        key = jax.random.key(seed)
        ks = jax.random.split(key, 12)
        s = 0.02
        x = jax.random.normal(ks[0], (4, 256, D_MODEL), dtype=jnp.float32)
        shared_w1 = jax.random.normal(ks[1], (D_FF, D_MODEL), dtype=jnp.float32) * s
        shared_b1 = jnp.zeros((D_FF,), dtype=jnp.float32)
        shared_w2 = jax.random.normal(ks[2], (D_MODEL, D_FF), dtype=jnp.float32) * s
        shared_b2 = jnp.zeros((D_MODEL,), dtype=jnp.float32)
        router_w = jax.random.normal(ks[3], (N_EXPERTS, D_MODEL), dtype=jnp.float32) * s
        router_b = jnp.zeros((N_EXPERTS,), dtype=jnp.float32)
        spec_w1 = jax.random.normal(ks[4], (N_EXPERTS, D_FF, D_MODEL), dtype=jnp.float32) * s
        spec_b1 = jnp.zeros((N_EXPERTS, D_FF), dtype=jnp.float32)
        spec_w2 = jax.random.normal(ks[5], (N_EXPERTS, D_MODEL, D_FF), dtype=jnp.float32) * s
        spec_b2 = jnp.zeros((N_EXPERTS, D_MODEL), dtype=jnp.float32)
        return dict(x=x, shared_w1=shared_w1, shared_b1=shared_b1, shared_w2=shared_w2, shared_b2=shared_b2, router_w=router_w, router_b=router_b, spec_w1=spec_w1, spec_b1=spec_b1, spec_w2=spec_w2, spec_b2=spec_b2)
    _L0_ffn_in = _L0_ffn_setup()
    _L0_c = _w((lambda *s: np.random.randn(*s).astype(np.float32) * 0.05)(8, 128))
    _L0_wmod = _w((lambda *s: np.random.randn(*s).astype(np.float32) * 0.05)(128, 6 * 128) * 128 ** (-0.5))

    def _L1_attn_setup():
        import jax, jax.numpy as jnp
        import numpy as np
        key = jax.random.key(seed)
        k1, k2, k3 = jax.random.split(key, 3)
        B, S, D, N = (2, 256, 128, 16)
        H = D // N
        x = jax.random.normal(k1, (B, S, D), dtype=jnp.float32)
        W_qkv = jax.random.normal(k2, (N, D, 3 * H), dtype=jnp.float32) / np.sqrt(D).astype(np.float32)
        W_out = jax.random.normal(k3, (N, H, D), dtype=jnp.float32) / np.sqrt(D).astype(np.float32)
        return {'x': x, 'W_qkv': W_qkv, 'W_out': W_out}
    _L1_attn_in = _L1_attn_setup()

    def _L1_ffn_setup():
        import jax, jax.numpy as jnp
        import numpy as np
        from jax import lax
        T, B, I, M, O = (32, 64, 128, 128, 128)

        def _xavier(key, shape):
            fan_out, fan_in = shape
            limit = float(np.sqrt(6.0 / (fan_in + fan_out)))
            return jax.random.uniform(key, shape, jnp.float32, -limit, limit)
        key = jax.random.key(seed)
        ks = jax.random.split(key, 9)
        x = jax.random.normal(ks[0], (T, B, I), jnp.float32)
        return {'x': x, 'wf': _xavier(ks[1], (M, I)), 'uf': _xavier(ks[2], (M, M)), 'bf': jnp.zeros((M,), jnp.float32), 'wi': _xavier(ks[3], (M, I)), 'ui': _xavier(ks[4], (M, M)), 'bi': jnp.zeros((M,), jnp.float32), 'wc': _xavier(ks[5], (M, I)), 'uc': _xavier(ks[6], (M, M)), 'bc': jnp.zeros((M,), jnp.float32), 'wo': _xavier(ks[7], (O, I)), 'uo': _xavier(ks[8], (O, M)), 'bo': jnp.zeros((O,), jnp.float32), 'in_c': jnp.zeros((M,), jnp.float32)}
    _L1_ffn_in = _L1_ffn_setup()
    _L1_c = _w((lambda *s: np.random.randn(*s).astype(np.float32) * 0.05)(8, 128))
    _L1_wmod = _w((lambda *s: np.random.randn(*s).astype(np.float32) * 0.05)(128, 6 * 128) * 128 ** (-0.5))
    _d = {'L0_attn_x': _L0_attn_in['x'], 'L0_ffn_shared_w1': _L0_ffn_in['shared_w1'], 'L0_ffn_shared_b1': _L0_ffn_in['shared_b1'], 'L0_ffn_shared_w2': _L0_ffn_in['shared_w2'], 'L0_ffn_shared_b2': _L0_ffn_in['shared_b2'], 'L0_ffn_router_w': _L0_ffn_in['router_w'], 'L0_ffn_router_b': _L0_ffn_in['router_b'], 'L0_ffn_spec_w1': _L0_ffn_in['spec_w1'], 'L0_ffn_spec_b1': _L0_ffn_in['spec_b1'], 'L0_ffn_spec_w2': _L0_ffn_in['spec_w2'], 'L0_ffn_spec_b2': _L0_ffn_in['spec_b2'], 'L0_c': _L0_c, 'L0_wmod': _L0_wmod, 'L1_attn_W_qkv': _L1_attn_in['W_qkv'], 'L1_attn_W_out': _L1_attn_in['W_out'], 'L1_ffn_wf': _L1_ffn_in['wf'], 'L1_ffn_uf': _L1_ffn_in['uf'], 'L1_ffn_bf': _L1_ffn_in['bf'], 'L1_ffn_wi': _L1_ffn_in['wi'], 'L1_ffn_ui': _L1_ffn_in['ui'], 'L1_ffn_bi': _L1_ffn_in['bi'], 'L1_ffn_wc': _L1_ffn_in['wc'], 'L1_ffn_uc': _L1_ffn_in['uc'], 'L1_ffn_bc': _L1_ffn_in['bc'], 'L1_ffn_wo': _L1_ffn_in['wo'], 'L1_ffn_uo': _L1_ffn_in['uo'], 'L1_ffn_bo': _L1_ffn_in['bo'], 'L1_ffn_in_c': _L1_ffn_in['in_c'], 'L1_c': _L1_c, 'L1_wmod': _L1_wmod}
    _x0 = _d['L0_attn_x']
    _d['L0_attn_x'] = jax.random.normal(jax.random.fold_in(jax.random.key(seed), 1), (8, 512, 128), dtype=_x0.dtype)
    del _x0
    return _d

def reference(L0_attn_x, L0_ffn_shared_w1, L0_ffn_shared_b1, L0_ffn_shared_w2, L0_ffn_shared_b2, L0_ffn_router_w, L0_ffn_router_b, L0_ffn_spec_w1, L0_ffn_spec_b1, L0_ffn_spec_w2, L0_ffn_spec_b2, L0_c, L0_wmod, L1_attn_W_qkv, L1_attn_W_out, L1_ffn_wf, L1_ffn_uf, L1_ffn_bf, L1_ffn_wi, L1_ffn_ui, L1_ffn_bi, L1_ffn_wc, L1_ffn_uc, L1_ffn_bc, L1_ffn_wo, L1_ffn_uo, L1_ffn_bo, L1_ffn_in_c, L1_c, L1_wmod):

    def _L0_attn_ref(x):
        import jax, jax.numpy as jnp
        import numpy as np
        EPS = 1e-08
        norms = jnp.linalg.norm(x, axis=-1)
        dots = jnp.einsum('bil,bjl->bij', x, x)
        sim = dots / jnp.maximum(norms[:, :, None] * norms[:, None, :], EPS)
        atten = jax.nn.softmax(sim, axis=-1)
        out = jnp.einsum('bij,bjl->bil', atten, x) + x
        return out

    def _L0_ffn_ref(x, shared_w1, shared_b1, shared_w2, shared_b2, router_w, router_b, spec_w1, spec_b1, spec_w2, spec_b2):
        import jax, jax.numpy as jnp
        import numpy as np
        D_MODEL = 128
        D_FF = 512
        N_EXPERTS = 8
        TOP_K = 2

        def _ffn(x, w1, b1, w2, b2):
            h = jax.nn.gelu(x @ w1.T + b1)
            return h @ w2.T + b2
        B, T, D = x.shape
        xf = x.reshape(-1, D)
        U = xf.shape[0]
        logits = xf @ router_w.T + router_b
        routing = jax.nn.softmax(logits, axis=-1)
        sel_w, sel_idx = jax.lax.top_k(routing, TOP_K)
        sel_w = sel_w / sel_w.sum(axis=-1, keepdims=True)
        comb = jnp.zeros_like(routing).at[jnp.arange(U)[:, None], sel_idx].set(sel_w)
        shared_out = _ffn(xf, shared_w1, shared_b1, shared_w2, shared_b2)

        def body(acc, params):
            w1, b1, w2, b2, we = params
            return (acc + we[:, None] * _ffn(xf, w1, b1, w2, b2), None)
        acc0 = jnp.zeros_like(shared_out)
        acc, _ = jax.lax.scan(body, acc0, (spec_w1, spec_b1, spec_w2, spec_b2, comb.T))
        return (shared_out + acc).reshape(B, T, D)

    def _L1_attn_ref(x, W_qkv, W_out):
        import jax, jax.numpy as jnp
        import numpy as np
        B, S, D = x.shape
        head_dim = W_qkv.shape[-1] // 3
        qkv = jnp.einsum('bsd,ndh->bnsh', x, W_qkv)
        q, k, v = jnp.split(qkv, 3, axis=-1)
        scale = jnp.asarray(1.0 / np.sqrt(head_dim), dtype=x.dtype)
        attn = jnp.einsum('bnqh,bnkh->bnqk', q, k) * scale
        mask = jnp.asarray(-10000000000.0, dtype=x.dtype) * (1.0 - jnp.tril(jnp.ones((S, S), dtype=x.dtype)))
        attn = jax.nn.softmax(attn + mask, axis=-1)
        out = jnp.einsum('bnqk,bnkh->bnqh', attn, v)
        out = out.reshape(B, -1, S)
        return jnp.einsum('bds,nhd->bsd', out, W_out)

    def _L1_ffn_ref(x, wf, uf, bf, wi, ui, bi, wc, uc, bc, wo, uo, bo, in_c):
        import jax, jax.numpy as jnp
        import numpy as np
        from jax import lax
        T, B, I, M, O = (32, 64, 128, 128, 128)

        def _xavier(key, shape):
            fan_out, fan_in = shape
            limit = float(np.sqrt(6.0 / (fan_in + fan_out)))
            return jax.random.uniform(key, shape, jnp.float32, -limit, limit)
        batch = x.shape[1]
        c0 = jnp.broadcast_to(in_c, (batch, in_c.shape[0]))

        def step(c, xt):
            ft = jax.nn.sigmoid(xt @ wf.T + c @ uf.T + bf)
            it = jax.nn.sigmoid(xt @ wi.T + c @ ui.T + bi)
            gt = jnp.tanh(xt @ wc.T + c @ uc.T + bc)
            c = ft * c + it * gt
            return (c, None)
        c_final, _ = lax.scan(step, c0, x)
        h = jnp.tanh(jnp.einsum('tbi,oi->tbo', x, wo) + c_final @ uo.T + bo)
        return h
    x = L0_attn_x
    mod = (_silu(L0_c) @ L0_wmod).reshape(L0_c.shape[0], 6, 1, -1)
    sa, ca, ga, sb, cb, gb = (mod[:, 0], mod[:, 1], mod[:, 2], mod[:, 3], mod[:, 4], mod[:, 5])
    ga = (2 * (ga >= 0) - 1) * jnp.maximum(jnp.abs(ga), 0.25)
    gb = (2 * (gb >= 0) - 1) * jnp.maximum(jnp.abs(gb), 0.25)
    h = _layernorm(x, axis=-1) * (1 + ca) + sa
    x = x + ga * _L0_attn_ref(h)
    h = _layernorm(x, axis=-1) * (1 + cb) + sb
    x = x + gb * _L0_ffn_ref(h, L0_ffn_shared_w1, L0_ffn_shared_b1, L0_ffn_shared_w2, L0_ffn_shared_b2, L0_ffn_router_w, L0_ffn_router_b, L0_ffn_spec_w1, L0_ffn_spec_b1, L0_ffn_spec_w2, L0_ffn_spec_b2)
    mod = (_silu(L1_c) @ L1_wmod).reshape(L1_c.shape[0], 6, 1, -1)
    sa, ca, ga, sb, cb, gb = (mod[:, 0], mod[:, 1], mod[:, 2], mod[:, 3], mod[:, 4], mod[:, 5])
    ga = (2 * (ga >= 0) - 1) * jnp.maximum(jnp.abs(ga), 0.25)
    gb = (2 * (gb >= 0) - 1) * jnp.maximum(jnp.abs(gb), 0.25)
    h = _layernorm(x, axis=-1) * (1 + ca) + sa
    x = x + ga * _L1_attn_ref(h, L1_attn_W_qkv, L1_attn_W_out)
    h = _layernorm(x, axis=-1) * (1 + cb) + sb
    x = x + gb * _L1_ffn_ref(h, L1_ffn_wf, L1_ffn_uf, L1_ffn_bf, L1_ffn_wi, L1_ffn_ui, L1_ffn_bi, L1_ffn_wc, L1_ffn_uc, L1_ffn_bc, L1_ffn_wo, L1_ffn_uo, L1_ffn_bo, L1_ffn_in_c)
    return x

_drawn_inputs = setup_inputs


def setup_inputs(seed=0):
    import zlib

    import numpy as np

    out = dict(_drawn_inputs(seed))
    spreads = {'L0_ffn_shared_b1': (0.0, 0.8),
     'L0_ffn_shared_b2': (0.0, 0.314),
     'L0_ffn_router_b': (0.0, 0.697),
     'L0_ffn_spec_b1': (0.0, 0.8),
     'L0_ffn_spec_b2': (0.0, 0.452),
     'L1_ffn_bf': (0.0, 0.8),
     'L1_ffn_bi': (0.0, 0.8),
     'L1_ffn_bc': (0.0, 0.544),
     'L1_ffn_bo': (0.0, 0.55),
     'L1_ffn_in_c': (0.0, 0.8)}
    factors = {'L0_ffn_shared_w1': 4.241,
     'L0_ffn_shared_w2': 3.838,
     'L0_ffn_router_w': 3.297,
     'L0_ffn_spec_w1': 6.122,
     'L0_ffn_spec_w2': 5.528,
     'L1_ffn_wf': 2.844,
     'L1_ffn_uf': 5.006,
     'L1_ffn_ui': 3.977}
    for name, (base, spread) in spreads.items():
        noise = np.random.default_rng([zlib.crc32(name.encode()), seed]).standard_normal(out[name].shape)
        drawn = base * np.exp(spread * noise) if base else spread * noise
        out[name] = jnp.asarray(drawn.astype(out[name].dtype))
    for name, factor in factors.items():
        out[name] = (out[name] * factor).astype(out[name].dtype)
    return out
```

```python
from contextlib import ExitStack

import numpy as np

import concourse.bass as bass
from concourse import mybir

F32 = mybir.dt.float32
BF16 = mybir.dt.bfloat16
ALU = mybir.AluOpType
ACT = mybir.ActivationFunctionType
AX_X = mybir.AxisListType.X

P = 128
NB = 8
S = 512
D = 128
NT = S // P
NE = 9
NR = NE - 1
FF = 512
NC = FF // P
NH = 16
HD = D // NH
LN_EPS = 1e-5
SIM_EPS = 1e-8
TINY = 1e-37
BIG = 1e30
NPART = 3
KROWS = NPART * NPART * HD
KMAX = KROWS + NPART
CAUSAL = sum((NT - k) * P for k in range(NT))
COL = [0, 512, 1024, 896]
MAX_UNITS = [(0, (0, 1, 2, 3)), (1, (0, 1, 2, 3)), (2, (0, 1)), (2, (2, 3)), (3, (0, 1)), (3, (2, 3))]
HOLD = 64


class Chain:

    def __init__(self, eng, sem):
        self.eng, self.sem, self.base, self.n = eng, sem, 0, 0

    def did(self, ins):
        ins.then_inc(self.sem, 1)
        self.n += 1

    def wait(self):
        self.eng.wait_ge(self.sem, self.base + self.n)

    def loop(self, b, per):
        self.start, self.per = self.base + self.n, per
        self.base, self.n = self.start + b * per, 0

    def end(self, count):
        assert self.n == self.per, (self.n, self.per)
        self.base, self.n = self.start + count * self.per, 0


def build(nc, ins, out, stop=None):
    ctx = ExitStack()
    with ctx:
        def sb(name, shape, dt=F32):
            return ctx.enter_context(nc.sbuf_tensor(name, shape, dt))

        def sem(name):
            return ctx.enter_context(nc.semaphore(name))

        def dram(name, shape, dt=F32):
            return nc.dram_tensor(name, shape, dt, kind="Internal").ap()

        modrow_d = dram("modrow_d", [NB, 4 * D])
        comb_d = dram("comb_d", [NR, S])
        q_d = dram("q_d", [NPART, D, S], BF16)
        k_d = dram("k_d", [NPART, D, S], BF16)
        mx_d = dram("mx_d", [NPART, NH * S], BF16)
        o_d = dram("o_d", [D, S])

        ident = sb("ident", [P, P])
        ident16 = sb("ident16", [P, P], BF16)
        ones = sb("ones", [P, P])
        mask16 = sb("mask16", [P, P], BF16)
        maskT16 = sb("maskT16", [P, P], BF16)
        rank = sb("rank", [P, NR])
        ones16 = sb("ones16", [NPART, S], BF16)
        maskf = sb("maskf", [P, 2, P])
        share1 = sb("share1", [P, 2 * NE * FF])
        share3 = sb("share3", [P, NB * 4 * D])
        share2 = sb("share2", [P, 3 * NT * S])

        def part(share, at, shape):
            n = int(np.prod(shape))
            v = share[:, at:at + n]
            if len(shape) == 2:
                v = v.rearrange("p (a b) -> p a b", a=shape[0])
            if len(shape) == 3:
                v = v.rearrange("p (a b c) -> p a b c", a=shape[0], b=shape[1])
            return v

        BC = part(share3, 0, [NB, 4, D])
        w1 = part(share1, 0, [NE, FF])
        w2 = part(share1, NE * FF, [NE, NC, D])
        b1 = sb("b1", [P, NE, NC])
        b2 = sb("b2", [P, NE])
        rw = sb("rw", [P, NR])
        rb = sb("rb", [P, NR])
        cT = sb("cT", [P, 2, NB])
        silu = sb("silu", [P, 2, NB])
        wmod = sb("wmod", [P, 2, 6, D])
        modT = sb("modT", [P, 2, 6, NB])
        gmag = sb("gmag", [P, 2, NB])
        modrow = sb("modrow", [NB, 4, D])
        rmag = sb("rmag", [NB, 2, D])
        wq = sb("wq", [P, 3, D])
        wout = sb("wout", [P, D])
        wsum = sb("wsum", [P, 1])
        yscale = sb("yscale", [P, NB])
        gw = sb("gw", [P, 8, D])
        gbias = sb("gbias", [P, 5])
        gbh = sb("gbh", [P, 2])
        half = sb("half", [P, NT])
        eps = sb("eps", [P, NT])
        tiny = sb("tiny", [P, NT])

        X = sb("X", [P, NB, NT, D])
        xs = sb("xs", [P, NT, D])
        stats = sb("stats", [P, NT, 6])
        mv = sb("mv", [P, NT, 2])
        rstd = sb("rstd", [P, NT])
        n_tok = sb("n_tok", [P, NT, D])
        h_tok = sb("h_tok", [P, NT, D])
        hT = sb("hT", [P, S])
        junk = sb("junk", [P, NT, D])
        n2 = sb("n2", [P, NT])
        rn = sb("rn", [P, NT])
        diag = sb("diag", [P, NT, P])
        R = part(share2, 0, [NT, S])
        sim = part(share2, NT * S, [NT, S])
        E = part(share2, 2 * NT * S, [NT, S])
        esum = sb("esum", [P, NT])
        rsum = sb("rsum", [P, NT])
        oT = sb("oT", [P, S])
        o_tok = sb("o_tok", [P, NT, D])
        h2T = sb("h2T", [P, S])
        L = sb("L", [P, NT, NR])
        Lb = sb("Lb", [P, NT, NR])
        key = sb("key", [P, NT, NR])
        sel1 = sb("sel1", [P, NT, NR])
        sel2 = sb("sel2", [P, NT, NR])
        m1 = sb("m1", [P, NT])
        m2 = sb("m2", [P, NT])
        r1 = sb("r1", [P, NT])
        dm = sb("dm", [P, NT])
        e2 = sb("e2", [P, NT])
        den = sb("den", [P, NT])
        w1st = sb("w1st", [P, NT])
        w2nd = sb("w2nd", [P, NT])
        comb = sb("comb", [P, NT, NR])
        combT = sb("combT", [NR, S])
        WB = sb("WB", [P, NR, S])
        g = sb("g", [P, 3, S])
        acc = sb("acc", [P, S])
        tmp = sb("tmp", [P, S])
        hB = sb("hB", [P, S])
        qf = part(share2, 0 * S, [S])
        kf = part(share2, 1 * S, [S])
        rest = part(share3, 0, [2, S])
        q3 = sb("q3", [P, NPART, S], BF16)
        k3 = sb("k3", [P, NPART, S], BF16)
        QST = sb("QST", [KMAX, NH, S], BF16)
        KST = sb("KST", [KMAX, NH, S], BF16)
        VA = part(share1, 0, [NT, NH, HOLD])
        nm = sb("nm", [P, 2, NH, NT])
        nmT = sb("nmT", [NH * NT, P])
        nrest = sb("nrest", [NH * NT, 2, P])
        nm3 = sb("nm3", [NH * NT, NPART, P], BF16)
        W = part(share1, NT * NH * HOLD, [2, CAUSAL])
        RD = part(share1, NT * NH * HOLD + 2 * CAUSAL, [2, S])
        OT = part(share1, NT * NH * HOLD + 2 * CAUSAL + 2 * S, [2, S])
        Z = part(share2, 2 * S, [S])
        zT = part(share2, 3 * S, [S])
        gates = part(share2, 8 * S, [3, S])
        cst = sb("cst", [P, S])
        ca_ = part(share2, 4 * S, [S])
        cb_ = part(share2, 5 * S, [S])
        XO = WB
        cu = part(share2, 6 * S, [S])
        pre = part(share2, 7 * S, [S])
        hout = sb("hout", [P, S])
        PS = ctx.enter_context(nc.psum_tensor("PS", [P, 8, 512], F32))

        s_ld, s_modrow, s_bc = sem("s_ld"), sem("s_modrow"), sem("s_bc")
        s_tanhc, s_silu, s_modps, s_modsb = sem("s_tanhc"), sem("s_silu"), sem("s_modps"), sem("s_modsb")
        s_dve, s_pool = sem("s_dve"), sem("s_pool")
        s_half = sem("s_half")
        names = ("stat rstd htok hTps hT n2 rn diag rbc dots sim E oT oTsb otok nTok h2ps h2T logit dm e2 comb"
                 " combTps combT combd wb gps gsb mm2 y yused acc zps").split()
        names += ("cst cast va h3ps h3 qps kps vps qf q3 k3 qkd qks vsb sc max nmps nm3 mxd mxs sT w pv po OT od Z zTs x3ps h4ps"
                  " h4 gps3 g3 xo c xops cups pre hth hg fps fin store").split()
        s = {n: sem("s_" + n) for n in names}

        block = ctx.enter_context(nc.Block())
        loads = [
            (cT[:, :, :], ins["cT"]), (wmod[:, :, :, :], ins["wmod"]), (ident[:, :], ins["ident"]),
            (X[:, :, :, :], ins["x"].rearrange("b (t p) d -> p b t d", p=P)),
            (ones[:, :], ins["ones"]), (rank[:, :], ins["rank"].broadcast_to([P, NR])),
            (w1[:, :, :], ins["w1"]), (w2[:, :, :, :], ins["w2"]), (b1[:, :, :], ins["b1"]), (b2[:, :], ins["b2"]),
            (rw[:, :], ins["rw"]), (rb[:, :], ins["rb"].broadcast_to([P, NR])),
        ]
        loads += [(wq[:, :, :], ins["wq"]), (wout[:, :], ins["wout"]), (gw[:, :, :], ins["gw"]),
                  (gbias[:, :], ins["gbias"]), (maskf[:, :, :], ins["mask"])]
        NLOAD = 16 * len(loads)

        @block.sync
        def _(sp):
            for dst, src in loads:
                sp.dma_start(dst, src).then_inc(s_ld, 16)
            sp.wait_ge(s_modsb, 3)
            sp.dma_start(modrow_d, modrow[:, :, :].rearrange("b k d -> b (k d)")).then_inc(s_modrow, 16)
            sp.wait_ge(s_modrow, 16)
            sp.dma_start(BC[:, :, :, :].rearrange("p b k d -> p (b k d)"),
                         modrow_d.rearrange("(o b) n -> o (b n)", o=1).broadcast_to([P, NB * 4 * D])).then_inc(s_bc, 16)
            with sp.Fori(0, NB) as b:
                sp.wait_ge(s["combT"], b + 1)
                sp.dma_start(comb_d, combT[:, :]).then_inc(s["combd"], 16)
                sp.wait_ge(s["combd"], 16 * b + 16)
                sp.dma_start(WB[:, :, :].rearrange("p e n -> p (e n)"),
                             comb_d.rearrange("(o e) n -> o (e n)", o=1).broadcast_to([P, NR * S])).then_inc(s["wb"], 16)
            if stop != "A":
                sp.wait_ge(s["cst"], 2)
                sp.dma_start(KST[KROWS:KMAX, :, :], ones16[:, :].unsqueeze(1).broadcast_to([NPART, NH, S])).then_inc(s["qks"], 16)
                with sp.Fori(0, NB) as b:
                    sp.wait_ge(s["q3"], b + 1)
                    sp.dma_start(q_d.rearrange("s p q -> p s q"), q3[:, :, :]).then_inc(s["qkd"], 16)
                    sp.wait_ge(s["k3"], b + 1)
                    sp.dma_start(k_d.rearrange("s p q -> p s q"), k3[:, :, :]).then_inc(s["qkd"], 16)
                    sp.wait_ge(s["qkd"], 32 * b + 32)
                    for sk in range(NPART):
                        for sq in range(NPART):
                            r0 = (sk * NPART + sq) * HD
                            for dst, src, part in ((QST, q_d, sq), (KST, k_d, sk)):
                                sp.dma_start(dst[r0:r0 + HD, :, :],
                                             src[part].rearrange("(n h) q -> h n q", h=HD)).then_inc(s["qks"], 16)
                    sp.wait_ge(s["nm3"], b + 1)
                    sp.dma_start(mx_d.rearrange("s (k q) -> k s q", q=P), nm3[:, :, :]).then_inc(s["mxd"], 16)
                    sp.wait_ge(s["mxd"], 16 * b + 16)
                    sp.dma_start(QST[KROWS:KMAX, :, :].rearrange("p n q -> p (n q)"), mx_d).then_inc(s["mxs"], 16)
                    sp.wait_ge(s["OT"], 2 * b + 2)
                    o_v = o_d.rearrange("(m c r) q -> c r m q", m=2, c=2)
                    for c in range(2):
                        sp.dma_start(o_v[c], OT[c * HOLD:c * HOLD + 32, :, :]).then_inc(s["od"], 16)
                    sp.wait_ge(s["od"], 32 * b + 32)
                    for n in range(NH):
                        sp.dma_start(Z[n * 8:n * 8 + 8, :].rearrange("a (h r) -> a h r", h=HD),
                                     o_d[n * HD:(n + 1) * HD, :].rearrange("h (a r) -> a h r", a=8)).then_inc(s["Z"], 16)
                if stop is None:
                    with sp.Fori(0, NB) as b:
                        sp.wait_ge(s["fin"], b + 1)
                        sp.dma_start(out[b].rearrange("(t p) d -> p t d", p=P), X[:, b, :, :]).then_inc(s["store"], 16)
                    sp.wait_ge(s["store"], 16 * NB)
                else:
                    sp.wait_ge(s["x3ps"], NB + 1)
                    sp.dma_start(out.rearrange("b (t p) d -> p b t d", p=P), X[:, :, :, :]).then_inc(s_ld, 16)
                    sp.wait_ge(s_ld, NLOAD + 16)
            if stop == "A":
                sp.wait_ge(s["acc"], NB + 1)
                sp.dma_start(out.rearrange("b (t p) d -> p b t d", p=P), X[:, :, :, :]).then_inc(s_ld, 16)
                sp.wait_ge(s_ld, NLOAD + 16)

        @block.gpsimd
        def _(pool):
            ch = Chain(pool, s_pool)
            pool.memset(half[:, :], -0.5)
            pool.memset(eps[:, :], LN_EPS)
            pool.memset(tiny[:, :], TINY)
            pool.memset(nm[:, :, :, :], 0.0).then_inc(s_half, 1)
            pool.wait_ge(s_half, 1)

            def inverse_root(dst, src, other, op, ready):
                ch.did(pool.tensor_tensor(dst, src, other, op))
                ch.wait()
                pool.tensor_tensor(dst, dst, half[:, :], ALU.pow).then_inc(ready, 1)

            with pool.Fori(0, NB) as b:
                ch.loop(b, 3)
                pool.wait_ge(s["stat"], 2 * b + 1)
                inverse_root(rstd[:, :], mv[:, :, 1], eps[:, :], ALU.add, s["rstd"])
                pool.wait_ge(s["n2"], b + 1)
                inverse_root(rn[:, :], n2[:, :], tiny[:, :], ALU.add, s["rn"])
                pool.wait_ge(s["stat"], 2 * b + 2)
                inverse_root(rstd[:, :], mv[:, :, 1], eps[:, :], ALU.add, s["rstd"])
                ch.end(NB)
            if stop == "A":
                return
            pool.memset(ones16[:, :], 1.0).then_inc(s["cst"], 1)
            pool.wait_ge(s["acc"], NB)
            ch.did(pool.memset(VA[:, :, :, :], 0.0))
            ch.wait()
            for j in range(4):
                i = pool.memset(VA[:, :, :, :].rearrange("p k (g j) c -> p k g j c", j=4)[:, :, :, j, 32 + j * HD:32 + (j + 1) * HD], 1.0)
            i.then_inc(s["cst"], 1)
            with pool.Fori(0, NB) as b:
                ch.loop(b, 2)
                for nth in (1, 2):
                    pool.wait_ge(s["stat"], 2 * NB + 2 * b + nth)
                    inverse_root(rstd[:, :], mv[:, :, 1], eps[:, :], ALU.add, s["rstd"])
                ch.end(NB)

        @block.scalar
        def _(act):
            act.wait_ge(s_ld, NLOAD)
            nc.scalar.activation(silu[:, :, :], cT[:, :, :], ACT.Tanh, scale=0.5).then_inc(s_tanhc, 1)
            with act.Fori(0, NB) as b:
                act.wait_ge(s["hTps"], b + 1)
                act.copy(hT[:, :], PS[:, 0, :]).then_inc(s["hT"], 1)
                for t in range(NT):
                    i = act.activation(junk[:, t, :], h_tok[:, t, :], ACT.Square, accum_out=n2[:, t:t + 1])
                i.then_inc(s["n2"], 1)
                for j in range(NT):
                    act.wait_ge(s["sim"], NT * b + j + 1)
                    act.activation(E[:, j, :], sim[:, j, :], ACT.Exp,
                                   accum_out=esum[:, j:j + 1]).then_inc(s["E"], 1)
                act.wait_ge(s["oT"], b + 1)
                act.copy(oT[:, :], PS[:, 6, :]).then_inc(s["oTsb"], 1)
                act.wait_ge(s["dm"], b + 1)
                act.activation(e2[:, :], dm[:, :], ACT.Exp).then_inc(s["e2"], 1)
                for i in range(NE * NC):
                    e, c = divmod(i, NC)
                    act.wait_ge(s["gps"], NE * NC * b + i + 1)
                    if i >= 3:
                        act.wait_ge(s["mm2"], NE * NC * b + i - 2)
                    act.activation(g[:, i % 3, :], PS[:, 2 + i % 3, :], ACT.Gelu_apprx_tanh,
                                   bias=b1[:, e, c:c + 1]).then_inc(s["gsb"], 1)
                    if i == NC:
                        act.wait_ge(s["combTps"], b + 1)
                        act.copy(combT[:, :], PS[0:NR, 7, :]).then_inc(s["combT"], 1)

            if stop == "A":
                return
            with act.Fori(0, NB) as b:
                act.wait_ge(s["qps"], b + 1)
                act.activation(qf[:, :], PS[:, 1, :], ACT.Copy, scale=float(HD) ** -0.5).then_inc(s["qf"], 1)
                act.wait_ge(s["kps"], b + 1)
                act.copy(kf[:, :], PS[:, 2, :]).then_inc(s["qf"], 1)
                for n in range(NH):
                    act.wait_ge(s["sT"], NH * b + n + 1)
                    if n >= 2:
                        act.wait_ge(s["pv"], NH * b + n - 1)
                    act.activation(W[:, n % 2, :], PS[:, 3 * (n % 2):3 * (n % 2) + 3, :].rearrange("p a q -> p (a q)")[:, 0:CAUSAL],
                                   ACT.Exp).then_inc(s["w"], 1)
                if stop == "B":
                    continue_ = False
                else:
                    for k in range(3):
                        act.wait_ge(s["gps3"], 4 * b + k + 1)
                        act.activation(gates[:, k, :], PS[:, 1 + k, :], ACT.Tanh, bias=gbh[:, k:k + 1] if k < 2 else gbias[:, 2:3],
                                       scale=0.5 if k < 2 else 1.0).then_inc(s["g3"], 1)
                    act.wait_ge(s["gps3"], 4 * b + 4)
                    act.activation(XO[:, b, :], PS[:, 4, :], ACT.Identity, bias=gbias[:, 3:4]).then_inc(s["xo"], 1)
            if stop == "B":
                return
            act.wait_ge(s["cups"], 1)
            act.copy(cu[:, :], PS[:, 1, :]).then_inc(s["cst"], 1)
            with act.Fori(0, NB) as b:
                act.wait_ge(s["pre"], b + 1)
                act.activation(hout[:, :], pre[:, :], ACT.Tanh).then_inc(s["hth"], 1)

        @block.tensor
        def _(pe):
            pe.wait_ge(s_ld, NLOAD)
            pe.wait_ge(s_silu, 1)
            for half_ in range(2):
                n0, n1 = (0, 4) if half_ == 0 else (4, 6)
                pe.matmul(PS[0:NB, half_, 0:(n1 - n0) * D], silu[:, 0, :], wmod[:, 0, n0:n1, :].rearrange("p k d -> p (k d)"), start=True, stop=True)
            for l in range(2):
                for k in range(6):
                    i = pe.matmul(PS[:, 2, (l * 6 + k) * NB:(l * 6 + k + 1) * NB], wmod[:, l, k, :], silu[:, l, :],
                                  start=True, stop=True)
            pe.matmul(PS[:, 2, 12 * NB:12 * NB + 1], wout[:, :], ones[:, 0:1], start=True, stop=True).then_inc(s_modps, 1)
            pe.wait_ge(s_modsb, 3)

            def transposes(bank, src, ready):
                for t in range(NT):
                    i = pe.transpose(PS[:, bank, t * P:(t + 1) * P], src[:, t, :], ident[:, :])
                i.then_inc(ready, 1)

            with pe.Fori(0, NB) as b:
                pe.wait_ge(s["htok"], b + 1)
                transposes(0, h_tok, s["hTps"])
                pe.wait_ge(s["hT"], b + 1)
                for j in range(NT):
                    pe.matmul(PS[:, 2 + j, :], hT[:, j * P:(j + 1) * P], hT[:, :], start=True,
                              stop=True).then_inc(s["dots"], 1)
                pe.wait_ge(s["diag"], b + 1)
                for t in range(NT):
                    i = pe.matmul(PS[:, 1, t * P:(t + 1) * P], ones[:, :], diag[:, t, :], start=True, stop=True)
                i.then_inc(s["rbc"], 1)
                for j in range(NT):
                    pe.wait_ge(s["E"], NT * b + j + 1)
                    i = pe.matmul(PS[:, 6, :], h_tok[:, j, :], E[:, j, :], start=(j == 0), stop=(j == NT - 1))
                i.then_inc(s["oT"], 1)
                pe.wait_ge(s["oTsb"], b + 1)
                transposes(0, oT[:, :].rearrange("p (t q) -> p t q", t=NT), s["otok"])
                pe.wait_ge(s["nTok"], b + 1)
                transposes(0, n_tok, s["h2ps"])
                pe.wait_ge(s["h2T"], b + 1)
                for t in range(NT):
                    i = pe.matmul(PS[:, 7, t * NR:(t + 1) * NR], h2T[:, t * P:(t + 1) * P], rw[:, :],
                                  start=True, stop=True)
                i.then_inc(s["logit"], 1)

                def mm1(i):
                    e, c = divmod(i, NC)
                    if i >= 3:
                        pe.wait_ge(s["gsb"], NE * NC * b + i - 2)
                    pe.matmul(PS[:, 2 + i % 3, :], w1[:, e, c * P:(c + 1) * P], h2T[:, :], start=True,
                              stop=True).then_inc(s["gps"], 1)

                def mm2(i):
                    e, c = divmod(i, NC)
                    pe.wait_ge(s["gsb"], NE * NC * b + i + 1)
                    if c == 0 and e >= 2:
                        pe.wait_ge(s["yused"], NE * b + e - 1)
                    pe.matmul(PS[:, 5 + e % 2, :], w2[:, e, c, :], g[:, i % 3, :], start=(c == 0),
                              stop=(c == NC - 1)).then_inc(s["mm2"], 1)

                for i in range(NE * NC):
                    mm1(i)
                    if i >= 2:
                        mm2(i - 2)
                    if i == NC:
                        pe.wait_ge(s["comb"], b + 1)
                        for t in range(NT):
                            q = pe.transpose(PS[0:NR, 7, t * P:(t + 1) * P], comb[:, t, :], ident[:, :])
                        q.then_inc(s["combTps"], 1)
                mm2(NE * NC - 2)
                mm2(NE * NC - 1)
                pe.wait_ge(s["acc"], b + 1)
                transposes(0, acc[:, :].rearrange("p (t q) -> p t q", t=NT), s["zps"])
            if stop == "A":
                return

            def tiles(v):
                return v[:, :].rearrange("p (t q) -> p t q", t=NT)

            with pe.Fori(0, NB) as b:
                pe.wait_ge(s["nTok"], NB + 2 * b + 1)
                transposes(0, n_tok, s["h3ps"])
                pe.wait_ge(s["h3"], b + 1)
                pe.matmul(PS[:, 1, :], wq[:, 0, :], hB[:, :], start=True, stop=True).then_inc(s["qps"], 1)
                pe.matmul(PS[:, 2, :], wq[:, 1, :], hB[:, :], start=True, stop=True).then_inc(s["kps"], 1)
                for t in range(NT):
                    i = pe.matmul(PS[:, 3, t * P:(t + 1) * P], hB[:, t * P:(t + 1) * P], wq[:, 2, :], start=True, stop=True)
                i.then_inc(s["vps"], 1)
                pe.wait_ge(s["qf"], 2 * b + 2)
                pe.wait_ge(s["vsb"], b + 1)
                pe.wait_ge(s["qks"], 18 * 16 * b + 18 * 16 + 16)
                for g4 in range(NH // 4):
                    for u, (t, heads) in enumerate(MAX_UNITS):
                        nth = g4 * len(MAX_UNITS) + u
                        if nth >= 2:
                            pe.wait_ge(s["max"], NH // 4 * len(MAX_UNITS) * b + nth - 1)
                        cols = (t + 1) * P
                        for i, n in enumerate(heads):
                            n += 4 * g4
                            bank, c0 = divmod(i * (cols if cols <= 256 else 512), 512)
                            bank += 2 + 2 * (nth % 2)
                            pe.matmul(PS[:, bank, c0:c0 + cols], QST[0:KROWS, n, t * P:(t + 1) * P], KST[0:KROWS, n, 0:cols],
                                      start=True, stop=False)
                            last = pe.matmul(PS[:, bank, c0 + t * P:c0 + cols], ident16[:, :], mask16[:, :],
                                             start=False, stop=True)
                        last.then_inc(s["sc"], 1)
                pe.wait_ge(s["max"], NH // 4 * len(MAX_UNITS) * (b + 1))
                pe.transpose(PS[:, 6, 0:P], nm[:, :, :, :].rearrange("p a n t -> p (a n t)"), ident[:, :]).then_inc(s["nmps"], 1)
                pe.wait_ge(s["mxs"], 16 * b + 16)

                def scores(n):
                    if n >= 2:
                        pe.wait_ge(s["w"], NH * b + n - 1)
                    for k in range(NT):
                        bank, c0 = divmod(COL[k], 512)
                        bank += 3 * (n % 2)
                        cols = (NT - k) * P
                        pe.matmul(PS[:, bank, c0:c0 + cols], KST[:, n, k * P:(k + 1) * P], QST[:, n, k * P:S],
                                  start=True, stop=False)
                        last = pe.matmul(PS[:, bank, c0:c0 + P], ident16[:, :], maskT16[:, :], start=False, stop=True)
                    last.then_inc(s["sT"], 1)

                def values(n):
                    pe.wait_ge(s["w"], NH * b + n + 1)
                    half_, rows = n // 8, HOLD * (n % 8 // 4)
                    for k in range(NT):
                        cols = (NT - k) * P
                        last = pe.matmul(PS[rows:rows + HOLD, 6 + half_, k * P:S], VA[:, k, n, :], W[:, n % 2, COL[k]:COL[k] + cols],
                                         start=(n % 4 == 0 and k == 0), stop=(n % 4 == 3 and k == NT - 1))
                    last.then_inc(s["pv"], 1)

                pe.wait_ge(s["nm3"], b + 1)
                for n in range(NH):
                    scores(n)
                    if n >= 1:
                        values(n - 1)
                values(NH - 1)
                pe.wait_ge(s["zTs"], b + 1)
                transposes(0, tiles(zT), s["x3ps"])
                if stop != "B":
                    pe.wait_ge(s["nTok"], NB + 2 * b + 2)
                    transposes(0, n_tok, s["h4ps"])
                    pe.wait_ge(s["h4"], b + 1)
                    for k in range(3):
                        pe.matmul(PS[:, 1 + k, :], gw[:, 2 * k, :], hB[:, :], start=True, stop=False)
                        pe.wait_ge(s["c"], b + 1)
                        pe.matmul(PS[:, 1 + k, :], gw[:, 2 * k + 1, :], cst[:, :], start=False, stop=True).then_inc(s["gps3"], 1)
                    pe.matmul(PS[:, 4, :], gw[:, 6, :], hB[:, :], start=True, stop=True).then_inc(s["gps3"], 1)
            if stop == "B":
                return
            pe.wait_ge(s["c"], NB + 1)
            pe.matmul(PS[:, 1, :], gw[:, 7, :], cst[:, :], start=True, stop=True).then_inc(s["cups"], 1)
            with pe.Fori(0, NB) as b:
                pe.wait_ge(s["hg"], b + 1)
                transposes(0, tiles(hout), s["fps"])

        @block.vector
        def _(dve):
            ch = Chain(dve, s_dve)
            dve.wait_ge(s_tanhc, 1)
            ch.did(dve.scalar_tensor_tensor(out=silu[:, :, :], in0=silu[:, :, :], scalar=1.0, in1=cT[:, :, :],
                                            op0=ALU.add, op1=ALU.mult))
            ch.wait()
            dve.tensor_scalar(silu[:, :, :], silu[:, :, :], 0.5, None, ALU.mult).then_inc(s_silu, 1)
            dve.wait_ge(s_modps, 1)
            ps_row = PS[0:NB, 0:2, :].rearrange("p a (k d) -> p (a k) d", d=D)

            def gate(dst, src, mag):
                ch.did(dve.tensor_scalar(dst, src, 0.0, 2.0, ALU.is_ge, ALU.mult))
                ch.wait()
                ch.did(dve.scalar_tensor_tensor(out=mag, in0=dst, scalar=-1.0, in1=src, op0=ALU.add, op1=ALU.mult))
                ch.wait()
                ch.did(dve.tensor_scalar(mag, mag, 0.25, None, ALU.max))
                ch.wait()
                return dve.scalar_tensor_tensor(out=dst, in0=dst, scalar=-1.0, in1=mag, op0=ALU.add, op1=ALU.mult)

            dve.tensor_copy(modrow[:, 0, :], ps_row[:, 0, :])
            dve.tensor_scalar(modrow[:, 1, :], ps_row[:, 1, :], 1.0, None, ALU.add)
            gate(modrow[:, 2, :], ps_row[:, 2, :], rmag[:, 0, :]).then_inc(s_modsb, 1)
            gate(modrow[:, 3, :], ps_row[:, 5, :], rmag[:, 1, :]).then_inc(s_modsb, 1)
            ps_T = PS[:, 2, 0:12 * NB].rearrange("p (l k b) -> p l k b", l=2, k=6)
            for k in (0, 3):
                dve.tensor_copy(modT[:, :, k, :], ps_T[:, :, k, :])
                ch.did(dve.tensor_scalar(modT[:, :, k + 1, :], ps_T[:, :, k + 1, :], 1.0, None, ALU.add))
                i = gate(modT[:, :, k + 2, :], ps_T[:, :, k + 2, :], gmag[:, :, :])
                if k == 0:
                    ch.did(i)
                    ch.wait()
                else:
                    i.then_inc(s_modsb, 1)
            dve.wait_ge(s_modsb, 3)
            ch.did(dve.tensor_copy(wsum[:, :], PS[:, 2, 12 * NB:12 * NB + 1]))
            ch.wait()
            ch.did(dve.tensor_scalar(yscale[:, :], modT[:, 1, 2, :], wsum[:, 0:1], None, ALU.mult))
            dve.tensor_copy(ident16[:, :], ident[:, :])
            dve.tensor_copy(mask16[:, :], maskf[:, 0, :])
            dve.tensor_copy(maskT16[:, :], maskf[:, 1, :])
            dve.tensor_scalar(gbh[:, :], gbias[:, 0:2], 0.5, None, ALU.mult)
            ch.did(dve.memset(cst[:, :], 0.0))
            ch.wait()
            dve.tensor_scalar(cst[:, :], cst[:, :], gbias[:, 4:5], None, ALU.add).then_inc(s["c"], 1)
            dve.wait_ge(s_bc, 16)

            def rows(k, b):
                return BC[:, b, k, :].unsqueeze(1).broadcast_to([P, NT, D])

            def layernorm(b, nth, ready, first=0):
                for t in range(NT):
                    dve.bn_stats(stats[:, t, :], xs[:, t, :])
                dve.drain()
                for t in range(NT):
                    i = dve.bn_aggr(mv[:, t, :], stats[:, t, :])
                i.then_inc(s["stat"], 1)
                dve.wait_ge(s["rstd"], first + 2 * b + nth)
                dve.wait_ge(s["stat"], first + 2 * b + nth)
                for t in range(NT):
                    i = dve.tensor_scalar(n_tok[:, t, :], xs[:, t, :], mv[:, t, 0:1], rstd[:, t:t + 1],
                                          ALU.subtract, ALU.mult)
                ch.did(i) if ready is None else i.then_inc(ready, 1)

            with dve.Fori(0, NB) as b:
                ch.loop(b, 34)
                ch.did(dve.tensor_scalar(xs[:, :, :], X[:, b, :, :], 1.0, None, ALU.mult))
                ch.wait()
                layernorm(b, 1, None)
                ch.wait()
                ch.did(dve.tensor_tensor(h_tok[:, :, :], n_tok[:, :, :], rows(1, b), ALU.mult))
                ch.wait()
                dve.tensor_tensor(h_tok[:, :, :], h_tok[:, :, :], rows(0, b), ALU.add).then_inc(s["htok"], 1)
                dve.wait_ge(s["rn"], b + 1)
                for t in range(NT):
                    i = dve.tensor_scalar(diag[:, t, :], ident[:, :], rn[:, t:t + 1], None, ALU.mult)
                i.then_inc(s["diag"], 1)
                dve.wait_ge(s["rbc"], b + 1)
                for j in range(NT):
                    i = dve.tensor_scalar(R[:, j, :], PS[:, 1, :], rn[:, j:j + 1], 1.0 / SIM_EPS, ALU.mult, ALU.min)
                ch.did(i)
                ch.wait()
                for j in range(NT):
                    dve.wait_ge(s["dots"], NT * b + j + 1)
                    dve.tensor_tensor(sim[:, j, :], PS[:, 2 + j, :], R[:, j, :], ALU.mult).then_inc(s["sim"], 1)
                dve.wait_ge(s["E"], NT * b + NT)
                ch.did(dve.reciprocal(rsum[:, :], esum[:, :]))
                dve.wait_ge(s["otok"], b + 1)
                ch.wait()
                for t in range(NT):
                    i = dve.scalar_tensor_tensor(out=o_tok[:, t, :], in0=PS[:, 0, t * P:(t + 1) * P],
                                                 scalar=rsum[:, t:t + 1], in1=h_tok[:, t, :], op0=ALU.mult, op1=ALU.add)
                ch.did(i)
                ch.wait()
                ch.did(dve.tensor_tensor(o_tok[:, :, :], o_tok[:, :, :], rows(2, b), ALU.mult))
                ch.wait()
                ch.did(dve.tensor_tensor(xs[:, :, :], xs[:, :, :], o_tok[:, :, :], ALU.add))
                ch.wait()
                layernorm(b, 2, s["nTok"])
                dve.wait_ge(s["h2ps"], b + 1)
                dve.tensor_scalar(h2T[:, :], PS[:, 0, :], modT[:, 0, 4, bass.ds(b, 1)], modT[:, 0, 3, bass.ds(b, 1)], ALU.mult,
                                  ALU.add).then_inc(s["h2T"], 1)
                ranks = rank[:, :].unsqueeze(1).broadcast_to([P, NT, NR])

                def each(v):
                    return v[:, :].unsqueeze(2).broadcast_to([P, NT, NR])

                def first_largest(sel, src, top):
                    ch.wait()
                    ch.did(dve.tensor_reduce(top[:, :], src[:, :, :], AX_X, ALU.max))
                    ch.wait()
                    ch.did(dve.tensor_tensor(key[:, :, :], src[:, :, :], each(top), ALU.is_equal))
                    ch.wait()
                    ch.did(dve.tensor_tensor(key[:, :, :], key[:, :, :], ranks, ALU.mult))
                    ch.wait()
                    ch.did(dve.tensor_reduce(r1[:, :], key[:, :, :], AX_X, ALU.max))
                    ch.wait()
                    ch.did(dve.tensor_tensor(sel[:, :, :], ranks, each(r1), ALU.is_equal))
                    ch.wait()

                dve.wait_ge(s["logit"], b + 1)
                ch.did(dve.tensor_tensor(L[:, :, :], PS[:, 7, 0:NT * NR].rearrange("p (t e) -> p t e", t=NT),
                                         rb[:, :].unsqueeze(1).broadcast_to([P, NT, NR]), ALU.add))
                first_largest(sel1, L, m1)
                ch.did(dve.scalar_tensor_tensor(out=Lb[:, :, :], in0=sel1[:, :, :], scalar=-BIG, in1=L[:, :, :],
                                                op0=ALU.mult, op1=ALU.add))
                first_largest(sel2, Lb, m2)
                dve.tensor_tensor(dm[:, :], m2[:, :], m1[:, :], ALU.subtract).then_inc(s["dm"], 1)
                dve.wait_ge(s["e2"], b + 1)
                ch.did(dve.tensor_scalar(den[:, :], e2[:, :], 1.0, None, ALU.add))
                ch.wait()
                ch.did(dve.reciprocal(w1st[:, :], den[:, :]))
                ch.wait()
                ch.did(dve.tensor_tensor(w2nd[:, :], e2[:, :], w1st[:, :], ALU.mult))
                ch.did(dve.tensor_tensor(sel1[:, :, :], sel1[:, :, :], each(w1st), ALU.mult))
                ch.wait()
                ch.did(dve.tensor_tensor(sel2[:, :, :], sel2[:, :, :], each(w2nd), ALU.mult))
                ch.wait()
                dve.tensor_tensor(comb[:, :, :], sel1[:, :, :], sel2[:, :, :], ALU.add).then_inc(s["comb"], 1)
                for e in range(NE):
                    dve.wait_ge(s["mm2"], NE * NC * b + NC * (e + 1))
                    if e == 0:
                        dve.tensor_scalar(acc[:, :], PS[:, 5, :], b2[:, 0:1], None, ALU.add).then_inc(s["yused"], 1)
                        dve.wait_ge(s["wb"], 16 * b + 16)
                    else:
                        ch.wait()
                        dve.scalar_tensor_tensor(out=tmp[:, :], in0=PS[:, 5 + e % 2, :], scalar=b2[:, e:e + 1],
                                                 in1=WB[:, e - 1, :], op0=ALU.add, op1=ALU.mult).then_inc(s["yused"], 1)
                        dve.wait_ge(s["yused"], NE * b + e + 1)
                        i = dve.tensor_tensor(acc[:, :], acc[:, :], tmp[:, :], ALU.add)
                        i.then_inc(s["acc"], 1) if e == NE - 1 else ch.did(i)
                dve.wait_ge(s["zps"], b + 1)
                ch.did(dve.tensor_tensor(o_tok[:, :, :], PS[:, 0, :].rearrange("p (t d) -> p t d", t=NT), rows(3, b),
                                         ALU.mult))
                ch.wait()
                ch.did(dve.tensor_tensor(X[:, b, :, :], xs[:, :, :], o_tok[:, :, :], ALU.add))
                ch.wait()
                ch.end(NB)
            if stop == "A":
                dve.memset(den[:, :], 0.0).then_inc(s["acc"], 1)
                return

            def split(parts, src, left, ready):
                ch.did(dve.tensor_copy(parts[:, 0, :], src))
                ch.wait()
                ch.did(dve.tensor_tensor(left[:, 0, :], src, parts[:, 0, :], ALU.subtract))
                ch.wait()
                ch.did(dve.tensor_copy(parts[:, 1, :], left[:, 0, :]))
                ch.wait()
                dve.tensor_tensor(parts[:, 2, :], left[:, 0, :], parts[:, 1, :], ALU.subtract).then_inc(ready, 1)

            with dve.Fori(0, NB) as b:
                ch.loop(b, 18)
                ch.did(dve.tensor_scalar(xs[:, :, :], X[:, b, :, :], 1.0, None, ALU.mult))
                ch.wait()
                layernorm(b, 1, s["nTok"], 2 * NB)
                dve.wait_ge(s["h3ps"], b + 1)
                dve.tensor_scalar(hB[:, :], PS[:, 0, :], modT[:, 1, 1, bass.ds(b, 1)], modT[:, 1, 0, bass.ds(b, 1)], ALU.mult,
                                  ALU.add).then_inc(s["h3"], 1)
                dve.wait_ge(s["qf"], 2 * b + 1)
                split(q3, qf[:, :], rest, s["q3"])
                dve.wait_ge(s["qf"], 2 * b + 2)
                dve.wait_ge(s["q3"], b + 1)
                split(k3, kf[:, :], rest, s["k3"])
                dve.wait_ge(s["vps"], b + 1)
                dve.wait_ge(s["cst"], 2)
                v_ps = PS[:, 3, :].rearrange("p (k g j h) -> p k g j h", k=NT, j=4, h=HD)
                va = VA[:, :, :, :].rearrange("p k (g j) c -> p k g j c", j=4)
                for j in range(4):
                    i = dve.tensor_copy(va[:, :, :, j, j * HD:(j + 1) * HD], v_ps[:, :, :, j, :])
                i.then_inc(s["vsb"], 1)
                for g4 in range(NH // 4):
                    for u, (t, heads) in enumerate(MAX_UNITS):
                        nth = g4 * len(MAX_UNITS) + u
                        dve.wait_ge(s["sc"], NH // 4 * len(MAX_UNITS) * b + nth + 1)
                        n0, k, cols = 4 * g4 + heads[0], len(heads), (t + 1) * P
                        src = PS[:, 2 + 2 * (nth % 2):4 + 2 * (nth % 2), :].rearrange("p a q -> p (a q)")
                        src = src[:, 0:k * max(cols, 512 if cols > 256 else cols)].rearrange("p (k q) -> p k q", k=k)[:, :, 0:cols]
                        dve.tensor_reduce(nm[:, 0, n0:n0 + k, t], src, AX_X, ALU.max, negate=True).then_inc(s["max"], 1)
                dve.wait_ge(s["nmps"], b + 1)
                ch.did(dve.tensor_copy(nmT[:, :], PS[0:NH * NT, 6, 0:P]))
                ch.wait()
                split(nm3, nmT[:, :], nrest, s["nm3"])
                dve.wait_ge(s["pv"], NH * b + NH)
                for c in range(2):
                    rows = slice(c * HOLD, c * HOLD + 32)
                    wrows = slice(c * HOLD + 32, c * HOLD + 64)
                    ch.did(dve.reciprocal(RD[rows, :, :], PS[wrows, 6:8, :]))
                    ch.wait()
                    dve.tensor_tensor(OT[rows, :, :], PS[rows, 6:8, :], RD[rows, :, :], ALU.mult).then_inc(s["OT"], 1)
                dve.wait_ge(s["Z"], 16 * NH * b + 16 * NH)
                dve.tensor_scalar(zT[:, :].rearrange("p (r h) -> p h r", h=HD), Z[:, :].rearrange("p (h r) -> p h r", h=HD),
                                  yscale[:, bass.ds(b, 1)], None, ALU.mult).then_inc(s["zTs"], 1)
                dve.wait_ge(s["x3ps"], b + 1)
                ch.did(dve.tensor_tensor(xs[:, :, :], xs[:, :, :], PS[:, 0, :].rearrange("p (t d) -> p t d", t=NT), ALU.add))
                ch.wait()
                ch.did(dve.tensor_scalar(X[:, b, :, :], xs[:, :, :], 1.0, None, ALU.mult))
                if stop != "B":
                    layernorm(b, 2, s["nTok"], 2 * NB)
                    dve.wait_ge(s["h4ps"], b + 1)
                    dve.tensor_scalar(hB[:, :], PS[:, 0, :], modT[:, 1, 4, bass.ds(b, 1)], modT[:, 1, 3, bass.ds(b, 1)], ALU.mult,
                                      ALU.add).then_inc(s["h4"], 1)
                    dve.wait_ge(s["g3"], 3 * b + 3)
                    ch.did(dve.scalar_tensor_tensor(out=ca_[:, :], in0=gates[:, 0, :], scalar=1.0, in1=cst[:, :], op0=ALU.add, op1=ALU.mult))
                    ch.did(dve.scalar_tensor_tensor(out=cb_[:, :], in0=gates[:, 1, :], scalar=1.0, in1=gates[:, 2, :], op0=ALU.add, op1=ALU.mult))
                    ch.wait()
                    ch.did(dve.tensor_tensor(ca_[:, :], ca_[:, :], cb_[:, :], ALU.add))
                    ch.wait()
                    dve.tensor_scalar(cst[:, :], ca_[:, :], 0.5, None, ALU.mult).then_inc(s["c"], 1)
                    dve.wait_ge(s["c"], b + 2)
                ch.end(NB)
            if stop == "B":
                dve.memset(den[:, :], 0.0).then_inc(s["x3ps"], 1)
                return
            dve.wait_ge(s["cst"], 3)
            dve.wait_ge(s["xo"], NB)
            with dve.Fori(0, NB) as b:
                ch.loop(b, 0)
                dve.tensor_tensor(pre[:, :], XO[:, b, :], cu[:, :], ALU.add).then_inc(s["pre"], 1)
                dve.wait_ge(s["hth"], b + 1)
                dve.tensor_scalar(hout[:, :], hout[:, :], modT[:, 1, 5, bass.ds(b, 1)], None, ALU.mult).then_inc(s["hg"], 1)
                dve.wait_ge(s["fps"], b + 1)
                dve.tensor_tensor(X[:, b, :, :], X[:, b, :, :], PS[:, 0, :].rearrange("p (t d) -> p t d", t=NT),
                                  ALU.add).then_inc(s["fin"], 1)
                ch.end(NB)


def host_layout(v):
    a = {k: np.asarray(x) for k, x in v.items()}
    w1 = np.concatenate([a["L0_ffn_shared_w1"][None], a["L0_ffn_spec_w1"]])
    w2 = np.concatenate([a["L0_ffn_shared_w2"][None], a["L0_ffn_spec_w2"]])
    b1 = np.concatenate([a["L0_ffn_shared_b1"][None], a["L0_ffn_spec_b1"]])
    b2 = np.concatenate([a["L0_ffn_shared_b2"][None], a["L0_ffn_spec_b2"]])
    wqkv = a["L1_attn_W_qkv"].reshape(NH, D, 3, HD)
    return {
        "x": a["L0_attn_x"],
        "cT": np.stack([a["L0_c"].T, a["L1_c"].T], 1),
        "wmod": np.stack([a["L0_wmod"], a["L1_wmod"]], 1).reshape(D, 2, 6, D),
        "w1": w1.transpose(2, 0, 1),
        "w2": w2.reshape(NE, D, NC, P).transpose(3, 0, 2, 1),
        "b1": b1.reshape(NE, NC, P).transpose(2, 0, 1),
        "b2": b2.T,
        "rw": a["L0_ffn_router_w"].T,
        "rb": a["L0_ffn_router_b"][None],
        "wq": wqkv.transpose(1, 2, 0, 3).reshape(D, 3, NH * HD),
        "wout": a["L1_attn_W_out"].reshape(NH * HD, D),
        "gw": np.stack([a["L1_ffn_" + n].T for n in ("wf", "uf", "wi", "ui", "wc", "uc", "wo", "uo")], 1),
        "gbias": np.stack([a["L1_ffn_" + n] for n in ("bf", "bi", "bc", "bo", "in_c")], 1),
        "mask": np.stack([np.triu(np.full((P, P), -1e10, np.float32), 1), np.tril(np.full((P, P), -1e10, np.float32), -1)], 1),
        "ident": np.eye(P, dtype=np.float32),
        "ones": np.ones((P, P), np.float32),
        "rank": np.arange(NR, 0, -1, dtype=np.float32)[None],
    }


def kernel(**inputs):
    import concourse.bacc as _bacc
    from concourse.bass_utils import run_bass_kernel_spmd as _run

    nc = _bacc.Bacc("TRN2", target_bir_lowering=False, num_devices=1)
    arrays, aps = {}, {}
    for name, a in host_layout(inputs).items():
        a = np.ascontiguousarray(a)
        arrays[f"in_{name}"] = a
        aps[name] = nc.dram_tensor(f"in_{name}", a.shape, mybir.dt.from_np(a.dtype), kind="ExternalInput").ap()
    out = nc.dram_tensor("out_0", (NB, S, D), F32, kind="ExternalOutput").ap()
    build(nc, aps, out)
    r = _run(nc, [arrays], core_ids=[0])
    return r.results[0]["out_0"]
```

```python
from contextlib import ExitStack

import numpy as np

import concourse.bass as bass
from concourse import mybir

F32 = mybir.dt.float32
F32R = mybir.dt.float32r
BF16 = mybir.dt.bfloat16
ALU = mybir.AluOpType
ACT = mybir.ActivationFunctionType
AX_X = mybir.AxisListType.X

P = 128
NB = 8
S = 512
D = 128
NT = S // P
NE = 9
NR = NE - 1
FF = 512
NC = FF // P
NU = NE * NC
VCH = (3,)
LAG = 3
RING = 6
NH = 16
HD = D // NH
LN_EPS = 1e-5
SIM_EPS = 1e-8
TINY = 1e-37
BIG = 1e30
NPART = 3
KROWS = NPART * NPART * HD
KMAX = KROWS + NPART
VW = 32
FG = 4
MAX_UNITS = [(0, (0, 1, 2, 3)), (1, (0, 1)), (1, (2, 3))] + [(t, (n,)) for t in (2, 3) for n in range(4)]
NM = NH // 4 * len(MAX_UNITS)
UNITS = [u for n in (0, 2) for u in (((n, 0, 0),), ((n, 1, 0), (n, 3, 3 * P)), ((n + 1, 0, 0),),
                                     ((n + 1, 1, 0), (n + 1, 3, 3 * P)), ((n, 2, 0), (n + 1, 2, 2 * P)))]
WHERE = {(n, k): (u, c) for u, pieces in enumerate(UNITS) for n, k, c in pieces}
UG = len(UNITS)
NV = NH // 4 * UG
C_LAG, C_H3, C_X3, C_Q, C_V, C_H4, C_G, C_MAX = 2, 1, 4, 5, 7, 11, (13, 14, 15, 17), 17
B_Q, B_K, B_GATES, D_REC = 5, 6, 15, 4
T_ROUTER, T_Z, T_H, T_COMB, T_NORM, T_DOTS, T_ATT, T_O, T_N = 0, 5, 6, 9, 11, 15, 20, 26, 31
V_START, V_ROUTE1, V_ROUTE2, V_TOK, V_Z, V_ROUTE3, V_DIAG, V_R, V_SIM, V_OUT, V_TOK2, V_MOD = (
    0, 1, 3, 4, 6, 7, 10, 14, 14, 26, 28, 31)
A_TH, A_HT, A_COMB, A_RBC, A_EXP, A_OT = 5, 7, 10, 10, 18, 24
P_RSTD1, P_NORM, P_RSTD2 = 0, 7, 27
Y_AT = 8


def wait_low(eng, s, b, i):
    e, c = divmod(i, NC)
    mine = [j for j in range(NC) if (j in VCH) == (c in VCH)]
    eng.wait_ge(s["glv" if c in VCH else "gl"], NE * len(mine) * b + len(mine) * e + mine.index(c) + 1)


class Chain:

    def __init__(self, eng, sem, per, start=0):
        self.eng, self.sem, self.per, self.start = eng, sem, per, start
        self.base, self.n = start, 0

    def batch(self, b):
        assert self.n in (0, self.per), (self.n, self.per)
        self.base, self.n = self.start + b * self.per, 0

    def did(self, ins):
        ins.then_inc(self.sem, 1)
        self.n += 1

    def wait(self):
        self.eng.wait_ge(self.sem, self.base + self.n)


def layer0(nc, ins, X, modT, dram):
    modrow_d, comb_d = dram("modrow_d", [NB, 4 * D]), dram("comb_d", [NR, S])
    with ExitStack() as ctx:
        def sb(name, shape, dt=F32):
            return ctx.enter_context(nc.sbuf_tensor(name, shape, dt))

        def sem(name):
            return ctx.enter_context(nc.semaphore("a_" + name))

        ident, ones, rank = sb("ident", [P, P]), sb("ones", [P, P]), sb("rank", [P, NR])
        w1h, w1l = sb("w1h", [P, NE, FF], F32R), sb("w1l", [P, NE, FF], F32R)
        w2h, w2l = sb("w2h", [P, NE, NC, D], F32R), sb("w2l", [P, NE, NC, D], F32R)
        b1, b2 = sb("b1", [P, NE, NC]), sb("b2", [P, NE])
        rw, rb = sb("rw", [P, NR]), sb("rb", [P, NR])
        cT, silu = sb("cT", [P, 2, NB]), sb("silu", [P, 2, NB])
        wmod = sb("wmod", [P, 2, 6, D])
        gmag = sb("gmag", [P, 2, NB])
        modrow, rmag = sb("modrow", [NB, 4, D]), sb("rmag", [NB, 2, D])
        BC = sb("BC", [P, NB, 4, D])
        half, eps, tiny = sb("half", [P, NT]), sb("eps", [P, NT]), sb("tiny", [P, NT])
        xs, x1 = sb("xs", [P, NT, D]), sb("x1", [P, NT, D])
        stats, mv, rstd = sb("stats", [P, NT, 6]), sb("mv", [P, NT, 2]), sb("rstd", [P, NT])
        n_tok, h_tok = sb("n_tok", [P, NT, D]), sb("h_tok", [P, NT, D])
        hT, rbc, oT = sb("hT", [P, S]), sb("rbc", [P, S]), sb("oT", [P, S])
        z_tok = oT[:, :].rearrange("p (t d) -> p t d", t=NT)
        n2, rn = sb("n2", [P, NT]), sb("rn", [P, NT])
        diag = sb("diag", [P, NT, P])
        R = sb("R", [P, NT, S])
        esum, rsum = sb("esum", [P, NT]), sb("rsum", [P, NT])
        h2T = sb("h2T", [P, S])
        h2h, h2l = sb("h2h", [P, S], F32R), sb("h2l", [P, S], F32R)
        L, Lb, key = sb("L", [P, NT, NR]), sb("Lb", [P, NT, NR]), sb("key", [P, NT, NR])
        sel1, sel2, comb = sb("sel1", [P, NT, NR]), sb("sel2", [P, NT, NR]), sb("comb", [P, NT, NR])
        m1, m2, r1, dm = sb("m1", [P, NT]), sb("m2", [P, NT]), sb("r1", [P, NT]), sb("dm", [P, NT])
        th, w1st, w2nd = sb("th", [P, NT]), sb("w1st", [P, NT]), sb("w2nd", [P, NT])
        combT = sb("combT", [NR, S])
        WB = sb("WB", [P, NR, S])
        stage = WB[:, 0:4, :].rearrange("p (a b) f -> p a b f", a=2)
        g = sb("g", [P, RING, S])
        gh, gl = sb("gh", [P, RING, S], F32R), sb("gl", [P, RING, S], F32R)
        acc, tmp = sb("acc", [P, S]), sb("tmp", [P, 2, S])
        PS = ctx.enter_context(nc.psum_tensor("PS", [P, 8, 512], F32))
        AUX = PS[:, 0, :]

        def dots_bank(j):
            return PS[:, 1 + j % 2, :]

        def g_bank(i):
            return PS[:, 3 + i % 3, :]

        def y_bank(e):
            return PS[:, 6 + e % 2, :]

        names = ("early weights modrow bc half tanhc silu modps modsb staged0 staged1 whi wlo x_in"
                 " dve_a dve_m pool_a stat rstd ntok htok hT_ps hT n2 rn diag rbc_ps rbc R dots sim E oT_ps oT"
                 " o_ps x1 n2tok h2_ps h2T split mm1 logit_ps top th comb combT_ps combT combd wb1 wb2"
                 " g gh gl glv mm2 y_used acc z_ps z_used x2").split()
        s = {n: sem(n) for n in names}
        block = ctx.enter_context(nc.Block())

        early = [(cT[:, :, :], ins["cT"]), (wmod[:, :, :, :], ins["wmod"]), (ident[:, :], ins["ident"]),
                 (ones[:, :], ins["ones"]), (rank[:, :], ins["rank"].broadcast_to([P, NR])),
                 (rw[:, :], ins["rw"]), (rb[:, :], ins["rb"].broadcast_to([P, NR]))]
        EARLY = 16 * len(early)

        @block.sync
        def _(sp):
            def load_x(b):
                sp.dma_start(xs[:, :, :], ins["x"][b].rearrange("(t p) d -> p t d", p=P)).then_inc(s["x_in"], 16)

            for dst, src in early[:2]:
                sp.dma_start(dst, src).then_inc(s["early"], 16)
            load_x(0)
            for dst, src in early[2:]:
                sp.dma_start(dst, src).then_inc(s["early"], 16)
            sp.wait_ge(s["modsb"], 2)
            sp.dma_start(modrow_d, modrow[:, :, :].rearrange("b k d -> b (k d)")).then_inc(s["modrow"], 16)
            sp.dma_start(b1[:, :, :], ins["b1"]).then_inc(s["weights"], 16)
            sp.dma_start(b2[:, :], ins["b2"]).then_inc(s["weights"], 16)
            sp.wait_ge(s["modrow"], 16)
            sp.dma_start(BC[:, :, :, :].rearrange("p b k d -> p (b k d)"),
                         modrow_d.rearrange("(o b) n -> o (b n)", o=1).broadcast_to([P, NB * 4 * D])).then_inc(s["bc"], 16)
            for e in range(NE):
                if e >= 2:
                    sp.wait_ge(s["wlo"], e - 1)
                sp.dma_start(stage[:, e % 2, 0, :], ins["w1"][:, e, :]).then_inc(s[f"staged{e % 2}"], 16)
                sp.dma_start(stage[:, e % 2, 1, :], ins["w2"][:, e, :]).then_inc(s[f"staged{e % 2}"], 16)

            def share_weights(b):
                sp.wait_ge(s["combT"], b + 1)
                sp.dma_start(comb_d, combT[:, :]).then_inc(s["combd"], 16)
                sp.wait_ge(s["combd"], 16 * b + 16)
                if isinstance(b, int) and b == 0:
                    sp.wait_ge(s["wlo"], NE)
                for part, lo, hi in (("wb1", 0, 2), ("wb2", 2, NR)):
                    sp.dma_start(WB[:, lo:hi, :].rearrange("p e n -> p (e n)"),
                                 comb_d[lo:hi].rearrange("(o e) n -> o (e n)", o=1).broadcast_to([P, (hi - lo) * S])
                                 ).then_inc(s[part], 16)

            sp.wait_ge(s["x1"], 1)
            load_x(1)
            share_weights(0)
            with sp.Fori(1, NB - 1) as b:
                sp.wait_ge(s["x1"], b + 1)
                load_x(b + 1)
                share_weights(b)
            share_weights(NB - 1)

        @block.gpsimd
        def _(pool):
            pool.memset(half[:, :], -0.5)
            pool.memset(eps[:, :], LN_EPS)
            pool.memset(tiny[:, :], TINY).then_inc(s["half"], 1)
            pool.wait_ge(s["half"], 1)
            ch = Chain(pool, s["pool_a"], 3)

            def inverse_root(dst, src, guard, ready):
                ch.did(pool.tensor_tensor(dst, src, guard, ALU.add))
                ch.wait()
                pool.tensor_tensor(dst, dst, half[:, :], ALU.pow).then_inc(ready, 1)

            def first_rstd(b):
                ch.batch(b)
                pool.wait_ge(s["stat"], 2 * b + 1)
                inverse_root(rstd[:, :], mv[:, :, 1], eps[:, :], s["rstd"])

            def norms(b):
                pool.wait_ge(s["n2"], b + 1)
                inverse_root(rn[:, :], n2[:, :], tiny[:, :], s["rn"])

            def second_rstd(b):
                pool.wait_ge(s["stat"], 2 * b + 2)
                inverse_root(rstd[:, :], mv[:, :, 1], eps[:, :], s["rstd"])

            def low_part(b, i):
                if i % NC in VCH:
                    return
                pool.wait_ge(s["gh"], NU * b + i + 1)
                pool.tensor_tensor(gl[:, i % RING, :], g[:, i % RING, :], gh[:, i % RING, :].bitcast(F32),
                                   ALU.subtract).then_inc(s["gl"], 1)

            def add_expert(b, e):
                if e >= 2:
                    pool.wait_ge(s["acc"], NR * b + e - 1)
                pool.wait_ge(s["y_used"], NE * b + e + 1)
                pool.tensor_tensor(acc[:, :], acc[:, :], tmp[:, e % 2, :], ALU.add).then_inc(s["acc"], 1)

            for e in range(NE):
                pool.wait_ge(s["whi"], 2 * e + 2)
                pool.tensor_tensor(w1l[:, e, :], stage[:, e % 2, 0, :], w1h[:, e, :].bitcast(F32), ALU.subtract)
                pool.tensor_tensor(w2l[:, e, :, :].rearrange("p c d -> p (c d)"), stage[:, e % 2, 1, :],
                                   w2h[:, e, :, :].rearrange("p c d -> p (c d)").bitcast(F32),
                                   ALU.subtract).then_inc(s["wlo"], 1)
                if e == 0:
                    first_rstd(0)
                if e == 2:
                    norms(0)
            second_rstd(0)

            def pair(b, after=True):
                for i in range(NU):
                    low_part(b, i)
                    if after:
                        if i == P_RSTD1:
                            first_rstd(b + 1)
                        if i == P_NORM:
                            norms(b + 1)
                        if i == P_RSTD2:
                            second_rstd(b + 1)
                    if i >= Y_AT + NC and (i - Y_AT) % NC == 1:
                        add_expert(b, (i - Y_AT) // NC)
                for e in range((NU - 2 - Y_AT) // NC + 1, NE):
                    add_expert(b, e)

            with pool.Fori(0, NB - 1) as b:
                pair(b)
            pair(NB - 1, False)

        @block.scalar
        def _(act):
            act.wait_ge(s["early"], EARLY)
            act.activation(silu[:, :, :], cT[:, :, :], ACT.Tanh, scale=0.5).then_inc(s["tanhc"], 1)

            def copy_hT(b):
                act.wait_ge(s["hT_ps"], b + 1)
                act.copy(hT[:, :], AUX).then_inc(s["hT"], 1)
                for t in range(NT):
                    i = act.activation(diag[:, t, :], h_tok[:, t, :], ACT.Square, accum_out=n2[:, t:t + 1])
                i.then_inc(s["n2"], 1)

            def copy_norms(b):
                act.wait_ge(s["rbc_ps"], b + 1)
                act.copy(rbc[:, :], AUX).then_inc(s["rbc"], 1)

            def exps(b):
                for j in range(NT):
                    act.wait_ge(s["sim"], NT * b + j + 1)
                    act.activation(R[:, j, :], R[:, j, :], ACT.Exp, accum_out=esum[:, j:j + 1]).then_inc(s["E"], 1)

            def copy_oT(b):
                act.wait_ge(s["oT_ps"], b + 1)
                act.copy(oT[:, :], AUX).then_inc(s["oT"], 1)

            def router_tanh(b):
                act.wait_ge(s["top"], b + 1)
                act.activation(th[:, :], dm[:, :], ACT.Tanh, scale=0.5).then_inc(s["th"], 1)

            def copy_combT(b):
                act.wait_ge(s["combT_ps"], b + 1)
                act.copy(combT[:, :], PS[0:NR, 1, :]).then_inc(s["combT"], 1)

            def gelu(b, i):
                e, c = divmod(i, NC)
                act.wait_ge(s["mm1"], NU * b + i + 1)
                if not (isinstance(b, int) and b == 0 and i < RING):
                    wait_low(act, s, b, i - RING) if i >= RING else wait_low(act, s, b - 1, i - RING + NU)
                act.activation(g[:, i % RING, :], g_bank(i), ACT.Gelu_apprx_tanh,
                               bias=b1[:, e, c:c + 1]).then_inc(s["g"], 1)

            for e in range(NE):
                act.wait_ge(s[f"staged{e % 2}"], 32 * (e // 2) + 32)
                act.copy(w1h[:, e, :], stage[:, e % 2, 0, :]).then_inc(s["whi"], 1)
                act.copy(w2h[:, e, :, :].rearrange("p c d -> p (c d)"), stage[:, e % 2, 1, :]).then_inc(s["whi"], 1)
                if e == 1:
                    copy_hT(0)
                if e == 3:
                    copy_norms(0)
                if e == 6:
                    exps(0)
            copy_oT(0)
            act.wait_ge(s["weights"], 32)

            def pair(b, after=True):
                for i in range(NU):
                    gelu(b, i)
                    if i == A_TH:
                        router_tanh(b)
                    if i == A_COMB:
                        copy_combT(b)
                    if after:
                        if i == A_HT:
                            copy_hT(b + 1)
                        if i == A_RBC:
                            copy_norms(b + 1)
                        if i == A_EXP:
                            exps(b + 1)
                        if i == A_OT:
                            copy_oT(b + 1)

            pair(0)
            with act.Fori(1, NB - 1) as b:
                pair(b)
            pair(NB - 1, False)

        @block.tensor
        def _(pe):
            pe.wait_ge(s["early"], EARLY)
            pe.wait_ge(s["silu"], 1)
            for bank, k0, k1 in ((1, 0, 4), (2, 4, 6)):
                pe.matmul(PS[0:NB, bank, 0:(k1 - k0) * D], silu[:, 0, :],
                          wmod[:, 0, k0:k1, :].rearrange("p k d -> p (k d)"), start=True, stop=True)
            for l in range(2):
                for k in range(6):
                    i = pe.matmul(PS[:, 3, (l * 6 + k) * NB:(l * 6 + k + 1) * NB], wmod[:, l, k, :], silu[:, l, :],
                                  start=True, stop=True)
            i.then_inc(s["modps"], 1)

            def transposes(src, ready, bank=0):
                for t in range(NT):
                    i = pe.transpose(PS[:, bank, t * P:(t + 1) * P], src[:, t, :], ident[:, :])
                i.then_inc(ready, 1)

            def transpose_h(b):
                pe.wait_ge(s["htok"], b + 1)
                transposes(h_tok, s["hT_ps"])

            def dots(b, j):
                pe.wait_ge(s["hT"], b + 1)
                if j >= 2:
                    pe.wait_ge(s["sim"], NT * b + j - 1)
                if j == 0 and not (isinstance(b, int) and b == 0):
                    pe.wait_ge(s["combT"], b)
                pe.matmul(dots_bank(j), hT[:, j * P:(j + 1) * P], hT[:, :], start=True, stop=True).then_inc(s["dots"], 1)

            def share_norms(b):
                pe.wait_ge(s["diag"], b + 1)
                pe.wait_ge(s["hT"], b + 1)
                for t in range(NT):
                    i = pe.matmul(PS[:, 0, t * P:(t + 1) * P], ones[:, :], diag[:, t, :], start=True, stop=True)
                i.then_inc(s["rbc_ps"], 1)

            def attend(b, j):
                pe.wait_ge(s["E"], NT * b + j + 1)
                i = pe.matmul(AUX, h_tok[:, j, :], R[:, j, :], start=(j == 0), stop=(j == NT - 1))
                if j == NT - 1:
                    i.then_inc(s["oT_ps"], 1)

            def transpose_o(b):
                pe.wait_ge(s["oT"], b + 1)
                transposes(oT[:, :].rearrange("p (t q) -> p t q", t=NT), s["o_ps"])

            def transpose_n(b):
                pe.wait_ge(s["n2tok"], b + 1)
                transposes(n_tok, s["h2_ps"])

            def router(b):
                pe.wait_ge(s["h2T"], b + 1)
                for t in range(NT):
                    i = pe.matmul(PS[:, 1, t * NR:(t + 1) * NR], h2T[:, t * P:(t + 1) * P], rw[:, :],
                                  start=True, stop=True)
                i.then_inc(s["logit_ps"], 1)

            def transpose_comb(b):
                pe.wait_ge(s["comb"], b + 1)
                for t in range(NT):
                    i = pe.transpose(PS[0:NR, 1, t * P:(t + 1) * P], comb[:, t, :], ident[:, :])
                i.then_inc(s["combT_ps"], 1)

            def transpose_z(b):
                pe.wait_ge(s["acc"], NR * b + NR)
                transposes(acc[:, :].rearrange("p (t q) -> p t q", t=NT), s["z_ps"], 2)

            def first_product(b, i):
                e, c = divmod(i, NC)
                if i == 0:
                    pe.wait_ge(s["split"], b + 1)
                if isinstance(b, int) and b == 0 and c == 0:
                    pe.wait_ge(s["wlo"], e + 1)
                if not (isinstance(b, int) and b == 0 and i < 3):
                    pe.wait_ge(s["g"], NU * b + i - 2)
                cols = slice(c * P, (c + 1) * P)
                pe.matmul(g_bank(i), w1h[:, e, cols], h2h[:, :], start=True, stop=False)
                pe.matmul(g_bank(i), w1h[:, e, cols], h2l[:, :], start=False, stop=False)
                pe.matmul(g_bank(i), w1l[:, e, cols], h2h[:, :], start=False, stop=True).then_inc(s["mm1"], 1)

            def second_product(b, i):
                e, c = divmod(i, NC)
                wait_low(pe, s, b, i)
                if c == 0 and not (isinstance(b, int) and b == 0 and e < 2):
                    pe.wait_ge(s["y_used"], NE * b + e - 1)
                hi, lo = gh[:, i % RING, :], gl[:, i % RING, :]
                pe.matmul(y_bank(e), w2h[:, e, c, :], hi, start=(c == 0), stop=False)
                pe.matmul(y_bank(e), w2h[:, e, c, :], lo, start=False, stop=False)
                pe.matmul(y_bank(e), w2l[:, e, c, :], hi, start=False, stop=(c == NC - 1)).then_inc(s["mm2"], 1)

            pe.wait_ge(s["modsb"], 3)
            transpose_h(0)
            share_norms(0)
            for j in range(NT):
                dots(0, j)
            pe.wait_ge(s["rbc"], 1)
            for j in range(NT):
                attend(0, j)
            transpose_o(0)
            transpose_n(0)
            def pair(b, before=True, after=True):
                for i in range(NU):
                    first_product(b, i)
                    if i >= LAG:
                        second_product(b, i - LAG)
                    if i == T_ROUTER:
                        router(b)
                    if i == T_COMB:
                        transpose_comb(b)
                    if before and i == T_Z:
                        transpose_z(b - 1)
                    if after:
                        if i == T_H:
                            transpose_h(b + 1)
                        if i == T_NORM:
                            share_norms(b + 1)
                        if T_DOTS <= i < T_DOTS + NT:
                            if before and i == T_DOTS + 1:
                                pe.wait_ge(s["z_used"], b)
                            dots(b + 1, i - T_DOTS)
                        if T_ATT <= i < T_ATT + NT:
                            if i == T_ATT:
                                pe.wait_ge(s["rbc"], b + 2)
                            attend(b + 1, i - T_ATT)
                        if i == T_O:
                            transpose_o(b + 1)
                        if i == T_N:
                            transpose_n(b + 1)
                for i in range(NU - LAG, NU):
                    second_product(b, i)

            pair(0, before=False)
            with pe.Fori(1, NB - 1) as b:
                pair(b)
            pair(NB - 1, after=False)
            transpose_z(NB - 1)

        @block.vector
        def _(dve):
            ch = Chain(dve, s["dve_a"], 7)
            first = Chain(dve, s["dve_m"], 0)
            dve.wait_ge(s["tanhc"], 1)
            first.did(dve.scalar_tensor_tensor(out=silu[:, :, :], in0=silu[:, :, :], scalar=1.0, in1=cT[:, :, :],
                                               op0=ALU.add, op1=ALU.mult))
            first.wait()
            dve.tensor_scalar(silu[:, :, :], silu[:, :, :], 0.5, None, ALU.mult).then_inc(s["silu"], 1)
            dve.wait_ge(s["modps"], 1)

            def gate(dst, src, mag):
                first.did(dve.tensor_scalar(dst, src, 0.0, 2.0, ALU.is_ge, ALU.mult))
                first.wait()
                first.did(dve.scalar_tensor_tensor(out=mag, in0=dst, scalar=-1.0, in1=src, op0=ALU.add, op1=ALU.mult))
                first.wait()
                first.did(dve.tensor_scalar(mag, mag, 0.25, None, ALU.max))
                first.wait()
                return dve.scalar_tensor_tensor(out=dst, in0=dst, scalar=-1.0, in1=mag, op0=ALU.add, op1=ALU.mult)

            ps_row = PS[0:NB, 1:3, :].rearrange("p a (k d) -> p (a k) d", d=D)
            dve.tensor_copy(modrow[:, 0, :], ps_row[:, 0, :])
            dve.tensor_scalar(modrow[:, 1, :], ps_row[:, 1, :], 1.0, None, ALU.add)
            gate(modrow[:, 2, :], ps_row[:, 2, :], rmag[:, 0, :]).then_inc(s["modsb"], 1)
            gate(modrow[:, 3, :], ps_row[:, 5, :], rmag[:, 1, :]).then_inc(s["modsb"], 1)
            ps_T = PS[:, 3, 0:12 * NB].rearrange("p (l k b) -> p l k b", l=2, k=6)
            for k in (0, 3):
                dve.tensor_copy(modT[:, :, k, :], ps_T[:, :, k, :])
                first.did(dve.tensor_scalar(modT[:, :, k + 1, :], ps_T[:, :, k + 1, :], 1.0, None, ALU.add))
                i = gate(modT[:, :, k + 2, :], ps_T[:, :, k + 2, :], gmag[:, :, :])
                if k == 0:
                    first.did(i)
                    first.wait()
                else:
                    i.then_inc(s["modsb"], 1)
            FIRST = first.n

            def rows(k, b):
                return BC[:, b, k, :].unsqueeze(1).broadcast_to([P, NT, D])

            def statistics(src):
                for t in range(NT):
                    dve.bn_stats(stats[:, t, :], src[:, t, :])
                dve.drain()
                for t in range(NT):
                    i = dve.bn_aggr(mv[:, t, :], stats[:, t, :])
                i.then_inc(s["stat"], 1)

            def normalize(src, nth, b):
                dve.wait_ge(s["rstd"], 2 * b + nth)
                dve.wait_ge(s["stat"], 2 * b + nth)
                for t in range(NT):
                    i = dve.tensor_scalar(n_tok[:, t, :], src[:, t, :], mv[:, t, 0:1], rstd[:, t:t + 1],
                                          ALU.subtract, ALU.mult)
                return i

            def start_tokens(b):
                ch.batch(b)
                dve.wait_ge(s["x_in"], 16 * b + 16)
                statistics(xs)

            def tokens(b):
                ch.did(normalize(xs, 1, b))
                ch.wait()
                ch.did(dve.tensor_tensor(h_tok[:, :, :], n_tok[:, :, :], rows(1, b), ALU.mult))
                ch.wait()
                dve.tensor_tensor(h_tok[:, :, :], h_tok[:, :, :], rows(0, b), ALU.add).then_inc(s["htok"], 1)

            def norm_diagonals(b):
                dve.wait_ge(s["rn"], b + 1)
                for t in range(NT):
                    i = dve.tensor_scalar(diag[:, t, :], ident[:, :], rn[:, t:t + 1], None, ALU.mult)
                i.then_inc(s["diag"], 1)

            def products_of_norms(b):
                dve.wait_ge(s["rbc"], b + 1)
                for j in range(NT):
                    i = dve.tensor_scalar(R[:, j, :], rbc[:, :], rn[:, j:j + 1], 1.0 / SIM_EPS, ALU.mult, ALU.min)
                i.then_inc(s["R"], 1)

            def similarities(b, j):
                dve.wait_ge(s["dots"], NT * b + j + 1)
                dve.wait_ge(s["R"], b + 1)
                dve.tensor_tensor(R[:, j, :], dots_bank(j), R[:, j, :], ALU.mult).then_inc(s["sim"], 1)

            def attention_out(b):
                dve.wait_ge(s["E"], NT * b + NT)
                ch.did(dve.reciprocal(rsum[:, :], esum[:, :]))
                dve.wait_ge(s["o_ps"], b + 1)
                ch.wait()
                for t in range(NT):
                    i = dve.scalar_tensor_tensor(out=n_tok[:, t, :], in0=PS[:, 0, t * P:(t + 1) * P],
                                                 scalar=rsum[:, t:t + 1], in1=h_tok[:, t, :], op0=ALU.mult, op1=ALU.add)
                ch.did(i)
                ch.wait()
                ch.did(dve.tensor_tensor(n_tok[:, :, :], n_tok[:, :, :], rows(2, b), ALU.mult))
                ch.wait()
                dve.tensor_tensor(x1[:, :, :], xs[:, :, :], n_tok[:, :, :], ALU.add).then_inc(s["x1"], 1)
                dve.wait_ge(s["x1"], b + 1)
                statistics(x1)
                ch.did(dve.tensor_scalar(X[:, b, :, :], x1[:, :, :], 1.0, None, ALU.mult))

            def second_tokens(b):
                normalize(x1, 2, b).then_inc(s["n2tok"], 1)

            def second_modulation(b):
                dve.wait_ge(s["h2_ps"], b + 1)
                dve.tensor_scalar(h2T[:, :], AUX, modT[:, 0, 4, bass.ds(b, 1)], modT[:, 0, 3, bass.ds(b, 1)], ALU.mult,
                                  ALU.add).then_inc(s["h2T"], 1)

            def split_h2(b):
                dve.wait_ge(s["h2T"], b + 1)
                if not (isinstance(b, int) and b == 0):
                    dve.wait_ge(s["mm1"], NU * b)
                ch.did(dve.tensor_copy(h2h[:, :], h2T[:, :]))
                ch.wait()
                dve.tensor_tensor(h2l[:, :], h2T[:, :], h2h[:, :].bitcast(F32), ALU.subtract).then_inc(s["split"], 1)

            ranks = rank[:, :].unsqueeze(1).broadcast_to([P, NT, NR])
            mo = Chain(dve, s["dve_m"], 1 + 5 + 1 + 5 + 3, FIRST)

            def each(v):
                return v[:, :].unsqueeze(2).broadcast_to([P, NT, NR])

            def first_largest(sel, src, top):
                mo.wait()
                mo.did(dve.tensor_reduce(top[:, :], src[:, :, :], AX_X, ALU.max))
                mo.wait()
                mo.did(dve.tensor_tensor(key[:, :, :], src[:, :, :], each(top), ALU.is_equal))
                mo.wait()
                mo.did(dve.tensor_tensor(key[:, :, :], key[:, :, :], ranks, ALU.mult))
                mo.wait()
                mo.did(dve.tensor_reduce(r1[:, :], key[:, :, :], AX_X, ALU.max))
                mo.wait()
                mo.did(dve.tensor_tensor(sel[:, :, :], ranks, each(r1), ALU.is_equal))

            def route_first(b):
                mo.batch(b)
                dve.wait_ge(s["logit_ps"], b + 1)
                mo.did(dve.tensor_tensor(L[:, :, :], PS[:, 1, 0:NT * NR].rearrange("p (t e) -> p t e", t=NT),
                                         rb[:, :].unsqueeze(1).broadcast_to([P, NT, NR]), ALU.add))
                first_largest(sel1, L, m1)

            def route_second(b):
                mo.wait()
                mo.did(dve.scalar_tensor_tensor(out=Lb[:, :, :], in0=sel1[:, :, :], scalar=-BIG, in1=L[:, :, :],
                                                op0=ALU.mult, op1=ALU.add))
                first_largest(sel2, Lb, m2)
                mo.wait()
                dve.tensor_tensor(dm[:, :], m1[:, :], m2[:, :], ALU.subtract).then_inc(s["top"], 1)

            def route_weights(b):
                dve.wait_ge(s["th"], b + 1)
                dve.tensor_scalar(w1st[:, :], th[:, :], 0.5, 0.5, ALU.mult, ALU.add)
                mo.did(dve.tensor_scalar(w2nd[:, :], th[:, :], -0.5, 0.5, ALU.mult, ALU.add))
                mo.wait()
                mo.did(dve.tensor_tensor(sel1[:, :, :], sel1[:, :, :], each(w1st), ALU.mult))
                mo.did(dve.tensor_tensor(sel2[:, :, :], sel2[:, :, :], each(w2nd), ALU.mult))
                mo.wait()
                dve.tensor_tensor(comb[:, :, :], sel1[:, :, :], sel2[:, :, :], ALU.add).then_inc(s["comb"], 1)

            def high_part(b, i):
                dve.wait_ge(s["g"], NU * b + i + 1)
                if not (isinstance(b, int) and b == 0 and i < RING):
                    dve.wait_ge(s["mm2"], NU * b + i - RING + 1)
                dve.tensor_copy(gh[:, i % RING, :], g[:, i % RING, :]).then_inc(s["gh"], 1)
                if i % NC in VCH:
                    dve.wait_ge(s["gh"], NU * b + i + 1)
                    dve.tensor_tensor(gl[:, i % RING, :], g[:, i % RING, :], gh[:, i % RING, :].bitcast(F32),
                                      ALU.subtract).then_inc(s["glv"], 1)

            def expert_out(b, e):
                dve.wait_ge(s["mm2"], NU * b + NC * (e + 1))
                if e == 0:
                    if not (isinstance(b, int) and b == 0):
                        dve.wait_ge(s["z_ps"], b)
                    dve.tensor_scalar(acc[:, :], y_bank(e), b2[:, 0:1], None, ALU.add).then_inc(s["y_used"], 1)
                    return
                dve.wait_ge(s["wb1"] if e <= 2 else s["wb2"], 16 * b + 16)
                if e >= 3:
                    dve.wait_ge(s["acc"], NR * b + e - 2)
                dve.scalar_tensor_tensor(out=tmp[:, e % 2, :], in0=y_bank(e), scalar=b2[:, e:e + 1],
                                         in1=WB[:, e - 1, :], op0=ALU.add, op1=ALU.mult).then_inc(s["y_used"], 1)

            def finish(b):
                dve.wait_ge(s["z_ps"], b + 1)
                dve.tensor_tensor(z_tok[:, :, :], PS[:, 2, :].rearrange("p (t d) -> p t d", t=NT), rows(3, b),
                                  ALU.mult).then_inc(s["z_used"], 1)
                dve.wait_ge(s["z_used"], b + 1)
                dve.tensor_tensor(X[:, b, :, :], X[:, b, :, :], z_tok[:, :, :], ALU.add).then_inc(s["x2"], 1)

            dve.wait_ge(s["bc"], 16)
            dve.wait_ge(s["modsb"], 3)
            start_tokens(0)
            tokens(0)
            norm_diagonals(0)
            products_of_norms(0)
            for j in range(NT):
                similarities(0, j)
            attention_out(0)
            second_tokens(0)
            second_modulation(0)
            split_h2(0)

            def pair(b, before=True, after=True):
                for i in range(NU):
                    high_part(b, i)
                    if i == V_ROUTE1:
                        route_first(b)
                    if i == V_ROUTE2:
                        route_second(b)
                    if i == V_ROUTE3:
                        route_weights(b)
                    if before and i == V_Z:
                        finish(b - 1)
                    if after:
                        if i == V_START:
                            start_tokens(b + 1)
                        if i == V_TOK:
                            tokens(b + 1)
                        if i == V_DIAG:
                            norm_diagonals(b + 1)
                        if i == V_R:
                            products_of_norms(b + 1)
                        if V_SIM <= i < V_SIM + NT:
                            similarities(b + 1, i - V_SIM)
                        if i == V_OUT:
                            attention_out(b + 1)
                        if i == V_TOK2:
                            second_tokens(b + 1)
                        if i == V_MOD:
                            second_modulation(b + 1)
                    if i >= Y_AT and (i - Y_AT) % NC == 0:
                        expert_out(b, (i - Y_AT) // NC)
                for e in range((NU - 1 - Y_AT) // NC + 1, NE - 1):
                    expert_out(b, e)
                if after:
                    split_h2(b + 1)
                expert_out(b, NE - 1)

            pair(0, before=False)
            with dve.Fori(1, NB - 1) as b:
                pair(b)
            pair(NB - 1, after=False)
            finish(NB - 1)


def layer1(nc, ins, out, X, modT, dram):
    q_d, k_d = dram("q_d", [NPART, HD, NH, S], BF16), dram("k_d", [NPART, NPART, HD, NH, S], BF16)
    mx_d, o_d = dram("mx_d", [NPART, NH * S], BF16), dram("o_d", [2, P, S])
    with ExitStack() as ctx:
        def sb(name, shape, dt=F32):
            return ctx.enter_context(nc.sbuf_tensor(name, shape, dt))

        def sem(name):
            return ctx.enter_context(nc.semaphore("b_" + name))

        eye, one, maskf = sb("eye", [P, P]), sb("one", [P, 1]), sb("maskf", [P, 2, P])
        eye16, mask16, maskT16 = sb("eye16", [P, P], BF16), sb("mask16", [P, P], BF16), sb("maskT16", [P, P], BF16)
        ones16 = sb("ones16", [NPART, S], BF16)
        wq, wout = sb("wq", [P, 3, D]), sb("wout", [P, D])
        wsum, yscale = sb("wsum", [P, 1]), sb("yscale", [P, NB])
        gw, gbias, gbh = sb("gw", [P, 8, D]), sb("gbias", [P, 5]), sb("gbh", [P, 2])
        half, eps = sb("halfb", [P, NT]), sb("epsb", [P, NT])
        stat3, mv3, rstd3 = sb("stat3", [P, NT, 6]), sb("mv3", [P, NT, 2]), sb("rstd3", [P, NT])
        n3 = sb("n3", [P, NT, D])
        h3 = sb("h3", [P, S])
        qf, kf, left = sb("qf", [P, S]), sb("kf", [P, S]), sb("left", [P, S])
        q3, k3 = sb("q3", [P, NPART, S], BF16), sb("k3", [P, NPART, S], BF16)
        QST, KST = sb("QST", [KMAX, 2, NH, S], BF16), sb("KST", [KMAX, 2, NH, S], BF16)
        VA = sb("VA", [P, 2, NT, NH, VW])
        nm = sb("nm", [P, 2, NH, NT])
        nmT, nleft = sb("nmT", [NH * NT, P]), sb("nleft", [NH * NT, P])
        nm3 = sb("nm3", [NH * NT, NPART, P], BF16)
        W = sb("W", [P, 2, UG, S])
        OT = sb("OT", [P, 2, S])
        Z, rz, zT = sb("Z", [P, HD + 1, S // HD]), sb("rz", [P, S // HD]), sb("zT", [P, S])
        stat4, mv4, rstd4 = sb("stat4", [P, NT, 6]), sb("mv4", [P, NT, 2]), sb("rstd4", [P, NT])
        n4 = sb("n4", [P, NT, D])
        h4 = sb("h4", [P, S])
        gates, cst = sb("gates", [P, 3, S]), sb("cst", [P, S])
        keep, new = sb("keep", [P, S]), sb("new", [P, S])
        XO, cu = sb("XO", [P, NB, S]), sb("cu", [P, S])
        PS = ctx.enter_context(nc.psum_tensor("PB", [P, 8, S], F32))
        B0, B1, B2 = PS[:, 0, :], PS[:, 1, :], PS[:, 2, :]
        OUT = (6, 7)

        names = ("loads wsum const eyes zero onesrow st3 rs3 n3 h3_ps h3 q_ps qf k_ps kf q3 k3 qd kd qst v_ps va sc mx nm_ps"
                 " nmT nm3 mxd mxs sT w pv po od z zT x3_ps x3 st4 rs4 n4 h4_ps h4 g_ps gate xo c cu_ps cu pre th hg"
                 " f_ps fin store pool_b dve_p dve_f dve_m dve_t").split()
        s = {n: sem(n) for n in names}
        block = ctx.enter_context(nc.Block())
        loads = [(eye[:, :], ins["ident"]), (wout[:, :], ins["wout"]),
                 (wq[:, :, :], ins["wq"]), (maskf[:, :, :], ins["mask"]), (gw[:, :, :], ins["gw"]),
                 (gbias[:, :], ins["gbias"])]
        LOADS = 16 * len(loads)

        def bodies(eng, body):
            body(0, 0, False, True)
            with eng.Fori(0, (NB - 2) // 2) as r:
                for k in range(2):
                    body(2 * r + k + 1, (k + 1) % 2, True, True)
            body(NB - 1, (NB - 1) % 2, True, False)

        @block.sync
        def _(sp):
            for dst, src in loads:
                sp.dma_start(dst, src).then_inc(s["loads"], 16)
            sp.wait_ge(s["const"], 1)
            for par in range(2):
                sp.dma_start(KST[KROWS:KMAX, par, :, :],
                             ones16[:, :].unsqueeze(1).broadcast_to([NPART, NH, S])).then_inc(s["onesrow"], 16)

            def stack(b, par):
                sp.wait_ge(s["q3"], b + 1)
                sp.dma_start(q_d.rearrange("s h n q -> (h n) s q"), q3[:, :, :]).then_inc(s["qd"], 16)
                sp.wait_ge(s["k3"], b + 1)
                for sq in range(NPART):
                    sp.dma_start(k_d[:, sq].rearrange("s h n q -> (h n) s q"), k3[:, :, :]).then_inc(s["kd"], 16)
                sp.wait_ge(s["qd"], 16 * b + 16)
                for sk in range(NPART):
                    sp.dma_start(QST[sk * NPART * HD:(sk + 1) * NPART * HD, par, :, :].rearrange("p n q -> p (n q)"),
                                 q_d.rearrange("s h n q -> (s h) (n q)")).then_inc(s["qst"], 16)
                sp.wait_ge(s["kd"], 48 * b + 48)
                sp.dma_start(KST[0:KROWS, par, :, :].rearrange("p n q -> p (n q)"),
                             k_d.rearrange("k s h n q -> (k s h) (n q)")).then_inc(s["qst"], 16)

            def share_maxima(b, par):
                sp.wait_ge(s["nm3"], b + 1)
                sp.dma_start(mx_d.rearrange("s (k q) -> k s q", q=P), nm3[:, :, :]).then_inc(s["mxd"], 16)
                sp.wait_ge(s["mxd"], 16 * b + 16)
                sp.dma_start(QST[KROWS:KMAX, par, :, :].rearrange("p n q -> p (n q)"), mx_d).then_inc(s["mxs"], 16)

            def reshape_out(b):
                sp.wait_ge(s["po"], b + 1)
                sp.dma_start(o_d.rearrange("a p q -> p a q"), OT[:, :, :]).then_inc(s["od"], 16)
                sp.wait_ge(s["od"], 16 * b + 16)
                for n in range(NH):
                    j, quad = divmod(n, 4)
                    bank, row = (0, 32 * quad + j * (HD + 1)) if j < 3 else (1, 32 * quad)
                    sp.dma_start(Z[n * HD:(n + 1) * HD, :, :],
                                 o_d[bank, row:row + HD + 1, :].rearrange("c (a r) -> a c r", a=HD)).then_inc(s["z"], 16)

            stack(0, 0)
            share_maxima(0, 0)

            def body(b, par, before, after):
                if after:
                    stack(b + 1, 1 - par)
                    share_maxima(b + 1, 1 - par)
                reshape_out(b)

            bodies(sp, body)
            with sp.Fori(0, NB // FG) as r:
                for k in range(FG):
                    sp.wait_ge(s["fin"], FG * r + k + 1)
                    sp.dma_start(out[FG * r + k].rearrange("(t p) d -> p t d", p=P),
                                 X[:, FG * r + k, :, :]).then_inc(s["store"], 16)
            sp.wait_ge(s["store"], 16 * NB)

        @block.gpsimd
        def _(pool):
            pool.memset(half[:, :], -0.5)
            pool.memset(eps[:, :], LN_EPS)
            pool.memset(one[:, :], 1.0)
            pool.memset(nm[:, :, :, :], 0.0)
            pool.memset(ones16[:, :], 1.0).then_inc(s["const"], 1)
            pool.memset(VA[:, :, :, :, :], 0.0).then_inc(s["zero"], 1)
            pool.wait_ge(s["zero"], 1)
            for j in range(4):
                c = (j % 3) * (HD + 1) + HD
                i = pool.memset(VA[:, :, :, 4 * j:4 * j + 4, c:c + 1].rearrange("p a k n o -> p (a k) (n o)"), 1.0)
            i.then_inc(s["zero"], 1)
            ch = Chain(pool, s["pool_b"], 1)
            ch4 = Chain(pool, s["dve_p"], 1)

            def inverse_root(ch, dst, src, ready):
                ch.did(pool.tensor_tensor(dst, src, eps[:, :], ALU.add))
                ch.wait()
                pool.tensor_tensor(dst, dst, half[:, :], ALU.pow).then_inc(ready, 1)

            def rstd_third(b):
                ch.batch(b)
                pool.wait_ge(s["st3"], b + 1)
                inverse_root(ch, rstd3[:, :], mv3[:, :, 1], s["rs3"])

            def rstd_fourth(b):
                ch4.batch(b)
                pool.wait_ge(s["st4"], b + 1)
                inverse_root(ch4, rstd4[:, :], mv4[:, :, 1], s["rs4"])

            pool.wait_ge(s["const"], 1)
            rstd_third(0)

            def body(b, par, before, after):
                if after:
                    rstd_third(b + 1)
                if before:
                    rstd_fourth(b - 1)

            bodies(pool, body)
            rstd_fourth(NB - 1)

        @block.scalar
        def _(act):
            act.wait_ge(s["loads"], LOADS)

            def copy_q(b):
                act.wait_ge(s["q_ps"], b + 1)
                act.activation(qf[:, :], B2, ACT.Copy, scale=float(HD) ** -0.5).then_inc(s["qf"], 1)

            def copy_k(b):
                act.wait_ge(s["k_ps"], b + 1)
                act.copy(kf[:, :], B0).then_inc(s["kf"], 1)

            def exps(b, v):
                j = v // UG
                act.wait_ge(s["sT"], NV * b + v + 1)
                if v % UG == 0 and not (isinstance(b, int) and b == 0 and j < 2):
                    act.wait_ge(s["pv"], 4 * b + j - 1)
                act.activation(W[:, j % 2, v % UG, :], PS[:, 3 + v % 3, :], ACT.Exp).then_inc(s["w"], 1)

            def copy_out(b):
                act.wait_ge(s["pv"], 4 * b + 4)
                act.copy(OT[:, 0, :], PS[:, OUT[0], :])
                act.copy(OT[:, 1, :], PS[:, OUT[1], :]).then_inc(s["po"], 1)

            def gates_of(b):
                for k in range(3):
                    act.wait_ge(s["g_ps"], 4 * b + k + 1)
                    act.activation(gates[:, k, :], PS[:, k, :], ACT.Tanh, bias=gbh[:, k:k + 1] if k < 2 else gbias[:, 2:3],
                                   scale=0.5 if k < 2 else 1.0).then_inc(s["gate"], 1)
                act.wait_ge(s["g_ps"], 4 * b + 4)
                act.activation(XO[:, b, :] if isinstance(b, int) else XO[:, b, :], B0, ACT.Identity,
                               bias=gbias[:, 3:4]).then_inc(s["xo"], 1)

            copy_q(0)
            copy_k(0)

            def body(b, par, before, after):
                for v in range(NV):
                    exps(b, v)
                    if after and v == B_Q:
                        copy_q(b + 1)
                    if after and v == B_K:
                        copy_k(b + 1)
                    if before and v == B_GATES:
                        gates_of(b - 1)
                copy_out(b)

            bodies(act, body)
            gates_of(NB - 1)
            act.wait_ge(s["cu_ps"], 1)
            act.copy(cu[:, :], PS[:, 4, :]).then_inc(s["cu"], 1)
            with act.Fori(0, NB // FG) as r:
                for k in range(FG):
                    act.wait_ge(s["pre"], FG * r + k + 1)
                    act.activation(W[:, 0, k, :], W[:, 0, k, :], ACT.Tanh).then_inc(s["th"], 1)

        @block.tensor
        def _(pe):
            pe.wait_ge(s["loads"], LOADS)
            pe.wait_ge(s["const"], 1)
            pe.matmul(PS[:, 0, 0:1], wout[:, :], one[:, :], start=True, stop=True).then_inc(s["wsum"], 1)

            def tiles(v):
                return v[:, :].rearrange("p (t q) -> p t q", t=NT)

            def transposes(bank, src, ready):
                for t in range(NT):
                    i = pe.transpose(bank[:, t * P:(t + 1) * P], src[:, t, :], eye[:, :])
                i.then_inc(ready, 1)

            def transpose_third(b):
                pe.wait_ge(s["n3"], b + 1)
                transposes(B0, n3, s["h3_ps"])

            def project_q(b):
                pe.wait_ge(s["h3"], b + 1)
                pe.matmul(B2, wq[:, 0, :], h3[:, :], start=True, stop=True).then_inc(s["q_ps"], 1)

            def project_k(b):
                pe.matmul(B0, wq[:, 1, :], h3[:, :], start=True, stop=True).then_inc(s["k_ps"], 1)

            def project_v(b):
                if not (isinstance(b, int) and b < 2):
                    pe.wait_ge(s["x3"], b - 1)
                for t in range(NT):
                    i = pe.matmul(B1[:, t * P:(t + 1) * P], h3[:, t * P:(t + 1) * P], wq[:, 2, :], start=True, stop=True)
                i.then_inc(s["v_ps"], 1)

            def row_scores(b, par, u):
                g4, (t, heads) = u // len(MAX_UNITS), MAX_UNITS[u % len(MAX_UNITS)]
                if u == 0:
                    pe.wait_ge(s["qst"], 64 * b + 64)
                if u >= 2:
                    pe.wait_ge(s["mx"], NM * b + u - 1)
                cols = (t + 1) * P
                for i, n in enumerate(heads):
                    n += 4 * g4
                    c0 = i * cols
                    bank = PS[:, 1 + u % 2, :]
                    pe.matmul(bank[:, c0:c0 + cols], QST[0:KROWS, par, n, t * P:(t + 1) * P], KST[0:KROWS, par, n, 0:cols],
                              start=True, stop=False)
                    last = pe.matmul(bank[:, c0 + t * P:c0 + cols], eye16[:, :], mask16[:, :], start=False, stop=True)
                last.then_inc(s["sc"], 1)

            def transpose_maxima(b):
                pe.wait_ge(s["mx"], NM * b + NM)
                pe.transpose(PS[:, 0, 0:P], nm[:, :, :, :].rearrange("p a n t -> p (a n t)"), eye[:, :]).then_inc(s["nm_ps"], 1)

            def scores(b, par, v):
                if v == 0:
                    pe.wait_ge(s["mxs"], 16 * b + 16)
                    if not (isinstance(b, int) and b == 0):
                        pe.wait_ge(s["w"], NV * b)
                elif v >= 3:
                    pe.wait_ge(s["w"], NV * b + v - 2)
                for n, k, c0 in UNITS[v % UG]:
                    n += 4 * (v // UG)
                    bank, cols = PS[:, 3 + v % 3, :], (NT - k) * P
                    pe.matmul(bank[:, c0:c0 + cols], KST[:, par, n, k * P:(k + 1) * P], QST[:, par, n, k * P:S],
                              start=True, stop=False)
                    last = pe.matmul(bank[:, c0:c0 + P], eye16[:, :], maskT16[:, :], start=False, stop=True)
                last.then_inc(s["sT"], 1)

            def values(b, par, j):
                pe.wait_ge(s["w"], NV * b + UG * (j + 1))
                if j in (0, 3) and not (isinstance(b, int) and b == 0):
                    pe.wait_ge(s["po"], b)
                if j == 0:
                    pe.wait_ge(s["va"], b + 1)
                for k in range(NT):
                    for quad in range(4):
                        u, c0 = WHERE[quad, k]
                        last = pe.matmul(PS[32 * quad:32 * quad + 32, OUT[j // 3], k * P:S], VA[:, par, k, 4 * j + quad, :],
                                         W[:, j % 2, u, c0:c0 + (NT - k) * P], start=(k == 0 and j in (0, 3)),
                                         stop=(k == NT - 1 and j >= 2))
                last.then_inc(s["pv"], 1)

            def transpose_out(b):
                pe.wait_ge(s["zT"], b + 1)
                transposes(B1, tiles(zT), s["x3_ps"])

            def transpose_fourth(b):
                pe.wait_ge(s["n4"], b + 1)
                transposes(B2, n4, s["h4_ps"])

            def gate_sums(b, k):
                if k == 0:
                    pe.wait_ge(s["h4"], b + 1)
                    pe.wait_ge(s["c"], b + 1)
                if k == 3:
                    pe.wait_ge(s["gate"], 3 * b + 1)
                    pe.matmul(B0, gw[:, 6, :], h4[:, :], start=True, stop=True).then_inc(s["g_ps"], 1)
                    return
                pe.matmul(PS[:, k, :], gw[:, 2 * k, :], h4[:, :], start=True, stop=False)
                pe.matmul(PS[:, k, :], gw[:, 2 * k + 1, :], cst[:, :], start=False, stop=True).then_inc(s["g_ps"], 1)

            pe.wait_ge(s["eyes"], 1)
            transpose_third(0)
            project_q(0)
            project_k(0)
            project_v(0)
            pe.wait_ge(s["onesrow"], 32)
            pe.wait_ge(s["va"], 1)
            for u in range(NM):
                row_scores(0, 0, u)
            transpose_maxima(0)

            def body(b, par, before, after):
                for v in range(NV):
                    scores(b, par, v)
                    if v >= UG and (v - C_LAG) % UG == UG - 1:
                        values(b, par, (v - C_LAG) // UG)
                    if after and v == C_H3:
                        transpose_third(b + 1)
                    if before and v == C_X3:
                        transpose_out(b - 1)
                    if after and v == C_Q:
                        project_q(b + 1)
                        project_k(b + 1)
                    if after and v == C_V:
                        project_v(b + 1)
                    if before and v == C_H4:
                        transpose_fourth(b - 1)
                    if before and v in C_G:
                        gate_sums(b - 1, C_G.index(v))
                    if after:
                        for u in range(NM):
                            if v == C_MAX + u // 2:
                                if before and u == 0:
                                    pe.wait_ge(s["gate"], 3 * b)
                                if u == 0:
                                    pe.wait_ge(s["va"], b + 2)
                                row_scores(b + 1, 1 - par, u)
                if after:
                    if before:
                        pe.wait_ge(s["xo"], b)
                    transpose_maxima(b + 1)
                values(b, par, 3)

            bodies(pe, body)
            transpose_out(NB - 1)
            transpose_fourth(NB - 1)
            for k in range(4):
                gate_sums(NB - 1, k)
            pe.wait_ge(s["c"], NB + 1)
            pe.matmul(PS[:, 4, :], gw[:, 7, :], cst[:, :], start=True, stop=True).then_inc(s["cu_ps"], 1)
            with pe.Fori(0, NB // FG) as r:
                for k in range(FG):
                    pe.wait_ge(s["hg"], FG * r + k + 1)
                    transposes(PS[:, k, :], W[:, 0, k, :].rearrange("p (t q) -> p t q", t=NT), s["f_ps"])

        @block.vector
        def _(dve):
            dve.wait_ge(s["loads"], LOADS)
            dve.tensor_copy(eye16[:, :], eye[:, :])
            dve.tensor_copy(mask16[:, :], maskf[:, 0, :])
            dve.tensor_copy(maskT16[:, :], maskf[:, 1, :])
            dve.tensor_scalar(gbh[:, :], gbias[:, 0:2], 0.5, None, ALU.mult).then_inc(s["eyes"], 1)
            dve.memset(cst[:, :], 0.0)
            dve.wait_ge(s["wsum"], 1)
            dve.tensor_copy(wsum[:, :], PS[:, 0, 0:1])
            dve.drain()
            dve.tensor_scalar(yscale[:, :], modT[:, 1, 2, :], wsum[:, 0:1], None, ALU.mult)
            dve.tensor_scalar(cst[:, :], cst[:, :], gbias[:, 4:5], None, ALU.add).then_inc(s["c"], 1)
            fr, mx = Chain(dve, s["dve_f"], 6), Chain(dve, s["dve_m"], 3)
            rec = Chain(dve, s["dve_t"], 3)

            def statistics(b, stats, mv, ready):
                for t in range(NT):
                    dve.bn_stats(stats[:, t, :], X[:, b, t, :])
                dve.drain()
                for t in range(NT):
                    i = dve.bn_aggr(mv[:, t, :], stats[:, t, :])
                i.then_inc(ready, 1)

            def normalize(b, dst, mv, rstd, ready):
                for t in range(NT):
                    i = dve.tensor_scalar(dst[:, t, :], X[:, b, t, :], mv[:, t, 0:1], rstd[:, t:t + 1],
                                          ALU.subtract, ALU.mult)
                i.then_inc(ready, 1)

            def split(ch, parts, src, left, ready):
                ch.did(dve.tensor_copy(parts[:, 0, :], src))
                ch.wait()
                ch.did(dve.tensor_tensor(left, src, parts[:, 0, :], ALU.subtract))
                ch.wait()
                ch.did(dve.tensor_copy(parts[:, 1, :], left))
                ch.wait()
                dve.tensor_tensor(parts[:, 2, :], left, parts[:, 1, :], ALU.subtract).then_inc(ready, 1)

            def normalize_third(b):
                dve.wait_ge(s["rs3"], b + 1)
                dve.wait_ge(s["st3"], b + 1)
                normalize(b, n3, mv3, rstd3, s["n3"])

            def modulate(b, dst, bank, k, come, ready):
                dve.wait_ge(come, b + 1)
                dve.tensor_scalar(dst[:, :], bank, modT[:, 1, k + 1, bass.ds(b, 1)], modT[:, 1, k, bass.ds(b, 1)],
                                  ALU.mult, ALU.add).then_inc(ready, 1)

            def split_q(b):
                fr.batch(b)
                dve.wait_ge(s["qf"], b + 1)
                split(fr, q3, qf[:, :], left[:, :], s["q3"])

            def split_k(b):
                dve.wait_ge(s["kf"], b + 1)
                dve.wait_ge(s["q3"], b + 1)
                split(fr, k3, kf[:, :], left[:, :], s["k3"])

            def place_values(b, par):
                dve.wait_ge(s["v_ps"], b + 1)
                v_ps = B1.rearrange("p (k n h) -> p k n h", k=NT, h=HD)
                for j in range(4):
                    c = (j % 3) * (HD + 1)
                    i = dve.tensor_copy(VA[:, par, :, 4 * j:4 * j + 4, c:c + HD], v_ps[:, :, 4 * j:4 * j + 4, :])
                i.then_inc(s["va"], 1)

            def maxima(b, u):
                g4, (t, heads) = u // len(MAX_UNITS), MAX_UNITS[u % len(MAX_UNITS)]
                dve.wait_ge(s["sc"], NM * b + u + 1)
                n0, k, cols = 4 * g4 + heads[0], len(heads), (t + 1) * P
                dve.tensor_reduce(nm[:, 0, n0:n0 + k, t], PS[:, 1 + u % 2, 0:k * cols].rearrange("p (k q) -> p k q", k=k),
                                  AX_X, ALU.max, negate=True).then_inc(s["mx"], 1)

            def split_maxima(b):
                dve.wait_ge(s["nm_ps"], b + 1)
                dve.tensor_copy(nmT[:, :], PS[0:NH * NT, 0, 0:P]).then_inc(s["nmT"], 1)
                mx.batch(b)
                dve.wait_ge(s["nmT"], b + 1)
                split(mx, nm3, nmT[:, :], nleft[:, :], s["nm3"])

            def scale_out(b):
                dve.wait_ge(s["z"], 16 * NH * b + 16 * NH)
                dve.reciprocal(rz[:, :], Z[:, HD, :])
                dve.drain()
                dve.scalar_tensor_tensor(out=zT[:, :].rearrange("p (r h) -> p h r", h=HD), in0=Z[:, 0:HD, :],
                                         scalar=yscale[:, bass.ds(b, 1)],
                                         in1=rz[:, :].unsqueeze(1).broadcast_to([P, HD, S // HD]),
                                         op0=ALU.mult, op1=ALU.mult).then_inc(s["zT"], 1)

            def add_attention(b):
                dve.wait_ge(s["x3_ps"], b + 1)
                dve.tensor_tensor(X[:, b, :, :], X[:, b, :, :], B1.rearrange("p (t d) -> p t d", t=NT),
                                  ALU.add).then_inc(s["x3"], 1)
                dve.drain()
                statistics(b, stat4, mv4, s["st4"])

            def normalize_fourth(b):
                dve.wait_ge(s["rs4"], b + 1)
                dve.wait_ge(s["st4"], b + 1)
                normalize(b, n4, mv4, rstd4, s["n4"])

            def recur(b):
                rec.batch(b)
                dve.wait_ge(s["gate"], 3 * b + 3)
                dve.wait_ge(s["g_ps"], 4 * b + 3)
                rec.did(dve.scalar_tensor_tensor(out=keep[:, :], in0=gates[:, 0, :], scalar=1.0, in1=cst[:, :], op0=ALU.add, op1=ALU.mult))
                rec.did(dve.scalar_tensor_tensor(out=new[:, :], in0=gates[:, 1, :], scalar=1.0, in1=gates[:, 2, :], op0=ALU.add, op1=ALU.mult))
                rec.wait()
                rec.did(dve.tensor_tensor(keep[:, :], keep[:, :], new[:, :], ALU.add))
                rec.wait()
                dve.tensor_scalar(cst[:, :], keep[:, :], 0.5, None, ALU.mult).then_inc(s["c"], 1)

            statistics(0, stat3, mv3, s["st3"])
            normalize_third(0)
            modulate(0, h3, B0, 0, s["h3_ps"], s["h3"])
            split_q(0)
            split_k(0)
            dve.wait_ge(s["zero"], 2)
            place_values(0, 0)
            for u in range(NM):
                maxima(0, u)
            split_maxima(0)

            def body(b, par, before, after):
                if after:
                    statistics(b + 1, stat3, mv3, s["st3"])
                if before and not after:
                    scale_out(b - 1)
                if after:
                    normalize_third(b + 1)
                if before and after:
                    scale_out(b - 1)
                if after:
                    modulate(b + 1, h3, B0, 0, s["h3_ps"], s["h3"])
                if before:
                    add_attention(b - 1)
                if after:
                    split_q(b + 1)
                    split_k(b + 1)
                if before:
                    normalize_fourth(b - 1)
                if after:
                    place_values(b + 1, 1 - par)
                if before:
                    modulate(b - 1, h4, B2, 3, s["h4_ps"], s["h4"])
                if after:
                    for u in range(NM):
                        maxima(b + 1, u)
                        if before and u == D_REC:
                            recur(b - 1)
                    split_maxima(b + 1)
                elif before:
                    recur(b - 1)

            bodies(dve, body)
            scale_out(NB - 1)
            add_attention(NB - 1)
            normalize_fourth(NB - 1)
            modulate(NB - 1, h4, B2, 3, s["h4_ps"], s["h4"])
            recur(NB - 1)
            dve.wait_ge(s["cu"], 1)
            dve.wait_ge(s["xo"], NB)
            with dve.Fori(0, NB // FG) as r:
                for k in range(FG):
                    b = FG * r + k
                    dve.tensor_tensor(W[:, 0, k, :], XO[:, b, :], cu[:, :], ALU.add).then_inc(s["pre"], 1)
                for k in range(FG):
                    b = FG * r + k
                    dve.wait_ge(s["th"], b + 1)
                    dve.tensor_scalar(W[:, 0, k, :], W[:, 0, k, :], modT[:, 1, 5, bass.ds(b, 1)], None,
                                      ALU.mult).then_inc(s["hg"], 1)
                for k in range(FG):
                    b = FG * r + k
                    dve.wait_ge(s["f_ps"], b + 1)
                    dve.tensor_tensor(X[:, b, :, :], X[:, b, :, :], PS[:, k, :].rearrange("p (t d) -> p t d", t=NT),
                                      ALU.add).then_inc(s["fin"], 1)


def build(nc, ins, out):
    with ExitStack() as ctx:
        X = ctx.enter_context(nc.sbuf_tensor("X", [P, NB, NT, D], F32))
        modT = ctx.enter_context(nc.sbuf_tensor("modT", [P, 2, 6, NB], F32))

        def dram(name, shape, dt=F32):
            return nc.dram_tensor(name, shape, dt, kind="Internal").ap()

        layer0(nc, ins, X, modT, dram)
        layer1(nc, ins, out, X, modT, dram)


def host_layout(v):
    a = {k: np.asarray(x) for k, x in v.items()}
    w1 = np.concatenate([a["L0_ffn_shared_w1"][None], a["L0_ffn_spec_w1"]])
    w2 = np.concatenate([a["L0_ffn_shared_w2"][None], a["L0_ffn_spec_w2"]])
    b1 = np.concatenate([a["L0_ffn_shared_b1"][None], a["L0_ffn_spec_b1"]])
    b2 = np.concatenate([a["L0_ffn_shared_b2"][None], a["L0_ffn_spec_b2"]])
    wqkv = a["L1_attn_W_qkv"].reshape(NH, D, 3, HD)
    return {
        "x": a["L0_attn_x"],
        "cT": np.stack([a["L0_c"].T, a["L1_c"].T], 1),
        "wmod": np.stack([a["L0_wmod"], a["L1_wmod"]], 1).reshape(D, 2, 6, D),
        "w1": w1.transpose(2, 0, 1),
        "w2": w2.reshape(NE, D, NC, P).transpose(3, 0, 2, 1),
        "b1": b1.reshape(NE, NC, P).transpose(2, 0, 1),
        "b2": b2.T,
        "rw": a["L0_ffn_router_w"].T,
        "rb": a["L0_ffn_router_b"][None],
        "wq": np.stack([wqkv[:, :, 0].transpose(1, 2, 0).reshape(D, NH * HD), wqkv[:, :, 1].transpose(1, 2, 0).reshape(D, NH * HD),
                        wqkv[:, :, 2].transpose(1, 0, 2).reshape(D, NH * HD)], 1),
        "wout": a["L1_attn_W_out"].reshape(NH * HD, D),
        "gw": np.stack([a["L1_ffn_" + n].T for n in ("wf", "uf", "wi", "ui", "wc", "uc", "wo", "uo")], 1),
        "gbias": np.stack([a["L1_ffn_" + n] for n in ("bf", "bi", "bc", "bo", "in_c")], 1),
        "mask": np.stack([np.triu(np.full((P, P), -1e10, np.float32), 1), np.tril(np.full((P, P), -1e10, np.float32), -1)], 1),
        "ident": np.eye(P, dtype=np.float32),
        "ones": np.ones((P, P), np.float32),
        "rank": np.arange(NR, 0, -1, dtype=np.float32)[None],
    }


def kernel(**inputs):
    import concourse.bacc as _bacc
    from concourse.bass_utils import run_bass_kernel_spmd as _run

    nc = _bacc.Bacc("TRN2", target_bir_lowering=False, num_devices=1)
    arrays, aps = {}, {}
    for name, a in host_layout(inputs).items():
        a = np.ascontiguousarray(a)
        arrays[f"in_{name}"] = a
        aps[name] = nc.dram_tensor(f"in_{name}", a.shape, mybir.dt.from_np(a.dtype), kind="ExternalInput").ap()
    out = nc.dram_tensor("out_0", (NB, S, D), F32, kind="ExternalOutput").ap()
    build(nc, aps, out)
    r = _run(nc, [arrays], core_ids=[0])
    return r.results[0]["out_0"]
```

```python
from contextlib import ExitStack

import numpy as np

import concourse.bass as bass
from concourse import mybir

F32 = mybir.dt.float32
F32R = mybir.dt.float32r
BF16 = mybir.dt.bfloat16
ALU = mybir.AluOpType
ACT = mybir.ActivationFunctionType
AX_X = mybir.AxisListType.X

P = 128
NB = 8
S = 512
D = 128
NT = S // P
STAGES = 4
NE = 9
NR = NE - 1
FF = 512
NC = FF // P
NU = NE * NC
VCH = (3,)
LAG = 4
RING = 6
NH = 16
HD = D // NH
LN_EPS = 1e-5
SIM_EPS = 1e-8
TINY = 1e-37
BIG = 1e30
NPART = 3
KROWS = NPART * NPART * HD
KMAX = KROWS + NPART
VW = 32
MAX_UNITS = [(0, (0, 1, 2, 3)), (1, (0, 1)), (1, (2, 3))] + [(t, (n,)) for t in (2, 3) for n in range(4)]
NM = NH // 4 * len(MAX_UNITS)
UNITS = [u for n in (0, 2) for u in (((n, 0, 0),), ((n, 1, 0), (n, 3, 3 * P)), ((n + 1, 0, 0),),
                                     ((n + 1, 1, 0), (n + 1, 3, 3 * P)), ((n, 2, 0), (n + 1, 2, 2 * P)))]
WHERE = {(n, k): (u, c) for u, pieces in enumerate(UNITS) for n, k, c in pieces}
UG = len(UNITS)
NV = NH // 4 * UG


def issued(v):
    return min(max(v - C_MAX + 1, 0) * NM // C_SPAN, NM)


C_LAG, C_V, C_H3, C_Q, C_K, C_X3, C_H4, C_G0, C_G1, C_G2, C_G3, C_OUT, C_NM = (
    2, 1, 4, 4, 7, 14, 21, 23, 24, 27, 30, 31, 39)
C_PART, C_MAX, C_SPAN = 3, 1, 36
D_Z, D_N4, D_GAP = 11, 21, 0
T_ROUTER, T_Z, T_H, T_COMB, T_NORM, T_DOTS, T_ATT, T_O, T_N = 2, 2, 6, 10, 11, 14, 19, 25, 31
V_START, V_ROUTE1, V_ROUTE2, V_TOK, V_Z, V_ROUTE3, V_DIAG, V_R, V_SIM, V_OUT, V_TOK2, V_MOD = (
    0, 1, 5, 4, 10, 7, 9, 13, 13, 25, 27, 31)
A_TH, A_HT, A_COMB, A_RBC, A_EXP, A_OT = 7, 7, 10, 10, 17, 23
P_RSTD1, P_NORM, P_RSTD2 = 0, 7, 26
Y_AT = 7


def wait_low(eng, s, b, i):
    e, c = divmod(i, NC)
    mine = [j for j in range(NC) if (j in VCH) == (c in VCH)]
    eng.wait_ge(s["glv" if c in VCH else "gl"], NE * len(mine) * b + len(mine) * e + mine.index(c) + 1)


class Chain:

    def __init__(self, eng, sem, per, start=0):
        self.eng, self.sem, self.per, self.start = eng, sem, per, start
        self.base, self.n = start, 0

    def batch(self, b):
        assert self.n in (0, self.per), (self.n, self.per)
        self.base, self.n = self.start + b * self.per, 0

    def did(self, ins):
        ins.then_inc(self.sem, 1)
        self.n += 1

    def wait(self):
        self.eng.wait_ge(self.sem, self.base + self.n)


def layer0(nc, ins, X, modT, ident, later, dram):
    modrow_d, comb_d = dram("modrow_d", [NB, 4 * D]), dram("comb_d", [NR, S])
    with ExitStack() as ctx:
        def sb(name, shape, dt=F32):
            return ctx.enter_context(nc.sbuf_tensor(name, shape, dt))

        def sem(name):
            return ctx.enter_context(nc.semaphore("a_" + name))

        ones, rank = sb("ones", [P, P]), sb("rank", [P, NR])
        w1h, w1l = sb("w1h", [P, NE, FF], F32R), sb("w1l", [P, NE, FF], F32R)
        w2h, w2l = sb("w2h", [P, NE, NC, D], F32R), sb("w2l", [P, NE, NC, D], F32R)
        b1, b2 = sb("b1", [P, NE, NC]), sb("b2", [P, NE])
        rw, rb = sb("rw", [P, NR]), sb("rb", [P, NR])
        cT, silu = sb("cT", [P, 2, NB]), sb("silu", [P, 2, NB])
        gmag = sb("gmag", [P, 2, NB])
        modrow, rmag = sb("modrow", [NB, 4, D]), sb("rmag", [NB, 2, D])
        BC = sb("BC", [P, NB, 4, D])
        half, eps, tiny = sb("half", [P, NT]), sb("eps", [P, NT]), sb("tiny", [P, NT])
        xs, x1 = sb("xs", [P, NT, D]), sb("x1", [P, NT, D])
        stats, mv, rstd = sb("stats", [P, NT, 6]), sb("mv", [P, NT, 2]), sb("rstd", [P, NT])
        n_tok, h_tok = sb("n_tok", [P, NT, D]), sb("h_tok", [P, NT, D])
        hT, rbc, oT = sb("hT", [P, S]), sb("rbc", [P, S]), sb("oT", [P, S])
        z_tok = oT[:, :].rearrange("p (t d) -> p t d", t=NT)
        n2, rn = sb("n2", [P, NT]), sb("rn", [P, NT])
        diag = sb("diag", [P, NT, P])
        R = sb("R", [P, NT, S])
        esum, rsum = sb("esum", [P, NT]), sb("rsum", [P, NT])
        h2T = sb("h2T", [P, S])
        h2h, h2l = sb("h2h", [P, S], F32R), sb("h2l", [P, S], F32R)
        L, Lb, key = sb("L", [P, NT, NR]), sb("Lb", [P, NT, NR]), sb("key", [P, NT, NR])
        sel1, sel2, comb = sb("sel1", [P, NT, NR]), sb("sel2", [P, NT, NR]), sb("comb", [P, NT, NR])
        m1, m2, r1, dm = sb("m1", [P, NT]), sb("m2", [P, NT]), sb("r1", [P, NT]), sb("dm", [P, NT])
        th, w1st, w2nd = sb("th", [P, NT]), sb("w1st", [P, NT]), sb("w2nd", [P, NT])
        combT = sb("combT", [NR, S])
        WB = sb("WB", [P, NR, S])
        stage = WB[:, :, :].rearrange("p (a b) f -> p a b f", a=STAGES)
        g = sb("g", [P, RING, S])
        wmod = g[:, 0:3, :].rearrange("p a f -> p (a f)").rearrange("p (l k d) -> p l k d", l=2, k=6)
        gh, gl = sb("gh", [P, RING, S], F32R), sb("gl", [P, RING, S], F32R)
        acc, tmp = sb("acc", [P, S]), sb("tmp", [P, 2, S])
        PS = ctx.enter_context(nc.psum_tensor("PS", [P, 8, 512], F32))
        AUX = PS[:, 0, :]

        def dots_bank(j):
            return PS[:, 1 + j % 2, :]

        def g_bank(i):
            return PS[:, 3 + i % 3, :]

        def y_bank(e):
            return PS[:, 6 + e % 2, :]

        names = ("later early weights modrow bc0 bc half tanhc silu modps modsb staged0 staged1 staged2 staged3"
                 " whi wlo1 wlo2 x_in tok_steps route_steps root_steps stat rstd htok hT_ps hT n2 rn diag"
                 " rbc_ps rbc R dots sim E oT_ps oT o_ps x1 n2tok h2_ps h2T split mm1 logit_ps top th comb"
                 " combT_ps combT combd wb1 wb2 g gh ghv gl glv mm2 y_used acc z_ps z_used").split()
        s = {n: sem(n) for n in names}
        block = ctx.enter_context(nc.Block())

        early = [(cT[:, :, :], ins["cT"]), (wmod, ins["wmod"]), (ident[:, :], ins["ident"]),
                 (ones[:, :], ins["ones"]), (rank[:, :], ins["rank"].broadcast_to([P, NR])),
                 (rw[:, :], ins["rw"]), (rb[:, :], ins["rb"].broadcast_to([P, NR]))]
        EARLY = 16 * len(early)

        @block.sync
        def _(sp):
            def load_x(b):
                sp.dma_start(xs[:, :, :], ins["x"][b].rearrange("(t p) d -> p t d", p=P)).then_inc(s["x_in"], 16)

            def load_weights(e):
                if e >= STAGES:
                    sp.wait_ge(s["wlo1"], e - STAGES + 1)
                    sp.wait_ge(s["wlo2"], e - STAGES + 1)
                sp.dma_start(stage[:, e % STAGES, 0, :], ins["w1"][:, e, :]).then_inc(s[f"staged{e % STAGES}"], 16)
                sp.dma_start(stage[:, e % STAGES, 1, :], ins["w2"][:, e, :]).then_inc(s[f"staged{e % STAGES}"], 16)

            def share_modulation(b0, b1, ready):
                sp.dma_start(BC[:, b0:b1, :, :].rearrange("p b k d -> p (b k d)"),
                             modrow_d[b0:b1].rearrange("(o b) n -> o (b n)", o=1).broadcast_to([P, (b1 - b0) * 4 * D])
                             ).then_inc(s[ready], 16)

            for dst, src in early[:3]:
                sp.dma_start(dst, src).then_inc(s["early"], 16)
            load_x(0)
            for dst, src in early[3:]:
                sp.dma_start(dst, src).then_inc(s["early"], 16)
            for e in range(STAGES):
                load_weights(e)
            sp.wait_ge(s["modsb"], 2)
            sp.dma_start(modrow_d, modrow[:, :, :].rearrange("b k d -> b (k d)")).then_inc(s["modrow"], 16)
            sp.dma_start(b1[:, :, :], ins["b1"]).then_inc(s["weights"], 16)
            sp.dma_start(b2[:, :], ins["b2"]).then_inc(s["weights"], 16)
            sp.wait_ge(s["modrow"], 16)
            share_modulation(0, 1, "bc0")
            for e in range(STAGES, NE):
                load_weights(e)
            share_modulation(1, NB, "bc")
            for dst, src in later:
                sp.dma_start(dst, src).then_inc(s["later"], 16)

            def share_weights(b):
                sp.wait_ge(s["combT"], b + 1)
                sp.dma_start(comb_d, combT[:, :]).then_inc(s["combd"], 16)
                sp.wait_ge(s["combd"], 16 * b + 16)
                if isinstance(b, int) and b == 0:
                    sp.wait_ge(s["wlo1"], NE)
                    sp.wait_ge(s["wlo2"], NE)
                for part, lo, hi in (("wb1", 0, 2), ("wb2", 2, NR)):
                    sp.dma_start(WB[:, lo:hi, :].rearrange("p e n -> p (e n)"),
                                 comb_d[lo:hi].rearrange("(o e) n -> o (e n)", o=1).broadcast_to([P, (hi - lo) * S])
                                 ).then_inc(s[part], 16)

            sp.wait_ge(s["x1"], 1)
            load_x(1)
            share_weights(0)
            with sp.Fori(1, NB - 1) as b:
                sp.wait_ge(s["x1"], b + 1)
                load_x(b + 1)
                share_weights(b)
            share_weights(NB - 1)
            sp.wait_ge(s["later"], 16 * len(later))

        @block.gpsimd
        def _(pool):
            pool.memset(half[:, :], -0.5)
            pool.memset(eps[:, :], LN_EPS)
            pool.memset(tiny[:, :], TINY).then_inc(s["half"], 1)
            pool.wait_ge(s["half"], 1)
            ch = Chain(pool, s["root_steps"], 3)

            def inverse_root(dst, src, guard, ready):
                ch.did(pool.tensor_tensor(dst, src, guard, ALU.add))
                ch.wait()
                pool.tensor_tensor(dst, dst, half[:, :], ALU.pow).then_inc(ready, 1)

            def first_rstd(b):
                ch.batch(b)
                pool.wait_ge(s["stat"], 2 * b + 1)
                inverse_root(rstd[:, :], mv[:, :, 1], eps[:, :], s["rstd"])

            def norms(b):
                pool.wait_ge(s["n2"], b + 1)
                inverse_root(rn[:, :], n2[:, :], tiny[:, :], s["rn"])

            def second_rstd(b):
                pool.wait_ge(s["stat"], 2 * b + 2)
                inverse_root(rstd[:, :], mv[:, :, 1], eps[:, :], s["rstd"])

            def low_part(b, i):
                if i % NC in VCH:
                    return
                mine = [c for c in range(NC) if c not in VCH]
                pool.wait_ge(s["gh"], NE * len(mine) * b + len(mine) * (i // NC) + mine.index(i % NC) + 1)
                pool.tensor_tensor(gl[:, i % RING, :], g[:, i % RING, :], gh[:, i % RING, :].bitcast(F32),
                                   ALU.subtract).then_inc(s["gl"], 1)

            def low_weights(e):
                pool.wait_ge(s["whi"], 2 * e + 1)
                pool.tensor_tensor(w1l[:, e, :], stage[:, e % STAGES, 0, :], w1h[:, e, :].bitcast(F32),
                                   ALU.subtract).then_inc(s["wlo1"], 1)

            first_rstd(0)
            for e in range(2):
                low_weights(e)
            norms(0)
            for e in range(2, 6):
                low_weights(e)
            second_rstd(0)
            for e in range(6, NE):
                low_weights(e)

            def pair(b, after=True):
                for i in range(NU):
                    low_part(b, i)
                    if after:
                        if i == P_RSTD1:
                            first_rstd(b + 1)
                        if i == P_NORM:
                            norms(b + 1)
                        if i == P_RSTD2:
                            second_rstd(b + 1)

            with pool.Fori(0, NB - 1) as b:
                pair(b)
            pair(NB - 1, False)

        @block.scalar
        def _(act):
            act.wait_ge(s["early"], EARLY)
            act.activation(silu[:, :, :], cT[:, :, :], ACT.Tanh, scale=0.5).then_inc(s["tanhc"], 1)

            def copy_hT(b):
                act.wait_ge(s["hT_ps"], b + 1)
                act.copy(hT[:, :], AUX).then_inc(s["hT"], 1)
                for t in range(NT):
                    i = act.activation(diag[:, t, :], h_tok[:, t, :], ACT.Square, accum_out=n2[:, t:t + 1])
                i.then_inc(s["n2"], 1)

            def copy_norms(b):
                act.wait_ge(s["rbc_ps"], b + 1)
                act.copy(rbc[:, :], AUX).then_inc(s["rbc"], 1)

            def exps(b):
                for j in range(NT):
                    act.wait_ge(s["sim"], NT * b + j + 1)
                    act.activation(R[:, j, :], R[:, j, :], ACT.Exp, accum_out=esum[:, j:j + 1]).then_inc(s["E"], 1)

            def copy_oT(b):
                act.wait_ge(s["oT_ps"], b + 1)
                act.copy(oT[:, :], AUX).then_inc(s["oT"], 1)

            def router_tanh(b):
                act.wait_ge(s["top"], b + 1)
                act.activation(th[:, :], dm[:, :], ACT.Tanh, scale=0.5).then_inc(s["th"], 1)

            def copy_combT(b):
                act.wait_ge(s["combT_ps"], b + 1)
                act.copy(combT[:, :], PS[0:NR, 1, :]).then_inc(s["combT"], 1)

            def gelu(b, i):
                e, c = divmod(i, NC)
                act.wait_ge(s["mm1"], NU * b + i + 1)
                if not (isinstance(b, int) and b == 0 and i < RING):
                    wait_low(act, s, b, i - RING) if i >= RING else wait_low(act, s, b - 1, i - RING + NU)
                act.activation(g[:, i % RING, :], g_bank(i), ACT.Gelu_apprx_tanh,
                               bias=b1[:, e, c:c + 1]).then_inc(s["g"], 1)

            def high_part(b, i):
                if i < 0 or i % NC in VCH:
                    return
                act.wait_ge(s["g"], NU * b + i + 1)
                if not (isinstance(b, int) and b == 0 and i < RING):
                    act.wait_ge(s["mm2"], NU * b + i - RING + 1)
                act.copy(gh[:, i % RING, :], g[:, i % RING, :]).then_inc(s["gh"], 1)

            def high_weights(e0, e1):
                for e in range(e0, e1):
                    act.wait_ge(s[f"staged{e % STAGES}"], 32 * (e // STAGES) + 32)
                    act.copy(w1h[:, e, :], stage[:, e % STAGES, 0, :]).then_inc(s["whi"], 1)
                    act.copy(w2h[:, e, :, :].rearrange("p c d -> p (c d)"), stage[:, e % STAGES, 1, :]).then_inc(s["whi"], 1)

            high_weights(0, 4)
            copy_hT(0)
            copy_norms(0)
            high_weights(4, 6)
            exps(0)
            high_weights(6, 7)
            copy_oT(0)
            high_weights(7, NE)
            act.wait_ge(s["weights"], 32)

            def pair(b, after=True):
                for i in range(NU):
                    gelu(b, i)
                    high_part(b, i - 1)
                    if i == A_TH:
                        router_tanh(b)
                    if i == A_COMB:
                        copy_combT(b)
                    if after:
                        if i == A_HT:
                            copy_hT(b + 1)
                        if i == A_RBC:
                            copy_norms(b + 1)
                        if i == A_EXP:
                            exps(b + 1)
                        if i == A_OT:
                            copy_oT(b + 1)

            pair(0)
            with act.Fori(1, NB - 1) as b:
                pair(b)
            pair(NB - 1, False)

        @block.tensor
        def _(pe):
            pe.wait_ge(s["early"], EARLY)
            pe.wait_ge(s["silu"], 1)
            for bank, k0, k1 in ((1, 0, 4), (2, 4, 6)):
                pe.matmul(PS[0:NB, bank, 0:(k1 - k0) * D], silu[:, 0, :],
                          wmod[:, 0, k0:k1, :].rearrange("p k d -> p (k d)"), start=True, stop=True)
            for l in range(2):
                for k in range(6):
                    i = pe.matmul(PS[:, 3, (l * 6 + k) * NB:(l * 6 + k + 1) * NB], wmod[:, l, k, :], silu[:, l, :],
                                  start=True, stop=True)
            i.then_inc(s["modps"], 1)

            def transposes(src, ready, bank=0):
                for t in range(NT):
                    i = pe.transpose(PS[:, bank, t * P:(t + 1) * P], src[:, t, :], ident[:, :])
                i.then_inc(ready, 1)

            def transpose_h(b):
                pe.wait_ge(s["htok"], b + 1)
                transposes(h_tok, s["hT_ps"])

            def dots(b, j):
                pe.wait_ge(s["hT"], b + 1)
                if j >= 2:
                    pe.wait_ge(s["sim"], NT * b + j - 1)
                if j == 0 and not (isinstance(b, int) and b == 0):
                    pe.wait_ge(s["combT"], b)
                pe.matmul(dots_bank(j), hT[:, j * P:(j + 1) * P], hT[:, :], start=True, stop=True).then_inc(s["dots"], 1)

            def share_norms(b):
                pe.wait_ge(s["diag"], b + 1)
                pe.wait_ge(s["hT"], b + 1)
                for t in range(NT):
                    i = pe.matmul(PS[:, 0, t * P:(t + 1) * P], ones[:, :], diag[:, t, :], start=True, stop=True)
                i.then_inc(s["rbc_ps"], 1)

            def attend(b, j):
                pe.wait_ge(s["E"], NT * b + j + 1)
                i = pe.matmul(AUX, h_tok[:, j, :], R[:, j, :], start=(j == 0), stop=(j == NT - 1))
                if j == NT - 1:
                    i.then_inc(s["oT_ps"], 1)

            def transpose_o(b):
                pe.wait_ge(s["oT"], b + 1)
                transposes(oT[:, :].rearrange("p (t q) -> p t q", t=NT), s["o_ps"])

            def transpose_n(b):
                pe.wait_ge(s["n2tok"], b + 1)
                transposes(n_tok, s["h2_ps"])

            def router(b):
                pe.wait_ge(s["h2T"], b + 1)
                for t in range(NT):
                    i = pe.matmul(PS[:, 1, t * NR:(t + 1) * NR], h2T[:, t * P:(t + 1) * P], rw[:, :],
                                  start=True, stop=True)
                i.then_inc(s["logit_ps"], 1)

            def transpose_comb(b):
                pe.wait_ge(s["comb"], b + 1)
                for t in range(NT):
                    i = pe.transpose(PS[0:NR, 1, t * P:(t + 1) * P], comb[:, t, :], ident[:, :])
                i.then_inc(s["combT_ps"], 1)

            def transpose_z(b):
                pe.wait_ge(s["acc"], NR * b + NR)
                transposes(acc[:, :].rearrange("p (t q) -> p t q", t=NT), s["z_ps"], 2)

            def first_product(b, i):
                e, c = divmod(i, NC)
                if i == 0:
                    pe.wait_ge(s["split"], b + 1)
                if isinstance(b, int) and b == 0 and c == 0:
                    pe.wait_ge(s["wlo1"], e + 1)
                if not (isinstance(b, int) and b == 0 and i < 3):
                    pe.wait_ge(s["g"], NU * b + i - 2)
                cols = slice(c * P, (c + 1) * P)
                pe.matmul(g_bank(i), w1h[:, e, cols], h2h[:, :], start=True, stop=False)
                pe.matmul(g_bank(i), w1h[:, e, cols], h2l[:, :], start=False, stop=False)
                pe.matmul(g_bank(i), w1l[:, e, cols], h2h[:, :], start=False, stop=True).then_inc(s["mm1"], 1)

            def second_product(b, i):
                e, c = divmod(i, NC)
                wait_low(pe, s, b, i)
                if isinstance(b, int) and b == 0 and c == 0:
                    pe.wait_ge(s["wlo2"], e + 1)
                if c == 0 and not (isinstance(b, int) and b == 0 and e < 2):
                    pe.wait_ge(s["y_used"], NE * b + max(e - 1, 0))
                hi, lo = gh[:, i % RING, :], gl[:, i % RING, :]
                pe.matmul(y_bank(e), w2h[:, e, c, :], hi, start=(c == 0), stop=False)
                pe.matmul(y_bank(e), w2h[:, e, c, :], lo, start=False, stop=False)
                pe.matmul(y_bank(e), w2l[:, e, c, :], hi, start=False, stop=(c == NC - 1)).then_inc(s["mm2"], 1)

            pe.wait_ge(s["modsb"], 3)
            transpose_h(0)
            share_norms(0)
            for j in range(NT):
                dots(0, j)
            pe.wait_ge(s["rbc"], 1)
            for j in range(NT):
                attend(0, j)
            transpose_o(0)
            transpose_n(0)
            def pair(b, before=True, after=True):
                for i in range(NU):
                    first_product(b, i)
                    if i >= LAG:
                        second_product(b, i - LAG)
                    if i == T_ROUTER:
                        router(b)
                    if i == T_COMB:
                        transpose_comb(b)
                    if before and i == T_Z:
                        transpose_z(b - 1)
                    if after:
                        if i == T_H:
                            transpose_h(b + 1)
                        if i == T_NORM:
                            share_norms(b + 1)
                        if T_DOTS <= i < T_DOTS + NT:
                            if before and i == T_DOTS + 1:
                                pe.wait_ge(s["z_used"], b)
                            dots(b + 1, i - T_DOTS)
                        if T_ATT <= i < T_ATT + NT:
                            if i == T_ATT:
                                pe.wait_ge(s["rbc"], b + 2)
                            attend(b + 1, i - T_ATT)
                        if i == T_O:
                            transpose_o(b + 1)
                        if i == T_N:
                            transpose_n(b + 1)
                for i in range(NU - LAG, NU):
                    second_product(b, i)

            pair(0, before=False)
            with pe.Fori(1, NB - 1) as b:
                pair(b)
            pair(NB - 1, after=False)
            transpose_z(NB - 1)

        @block.vector
        def _(dve):
            ch = Chain(dve, s["tok_steps"], 7)
            first = Chain(dve, s["route_steps"], 0)
            dve.wait_ge(s["tanhc"], 1)
            first.did(dve.scalar_tensor_tensor(out=silu[:, :, :], in0=silu[:, :, :], scalar=1.0, in1=cT[:, :, :],
                                               op0=ALU.add, op1=ALU.mult))
            first.wait()
            dve.tensor_scalar(silu[:, :, :], silu[:, :, :], 0.5, None, ALU.mult).then_inc(s["silu"], 1)
            dve.wait_ge(s["modps"], 1)

            def gate(dst, src, mag):
                first.did(dve.tensor_scalar(dst, src, 0.0, 2.0, ALU.is_ge, ALU.mult))
                first.wait()
                first.did(dve.scalar_tensor_tensor(out=mag, in0=dst, scalar=-1.0, in1=src, op0=ALU.add, op1=ALU.mult))
                first.wait()
                first.did(dve.tensor_scalar(mag, mag, 0.25, None, ALU.max))
                first.wait()
                return dve.scalar_tensor_tensor(out=dst, in0=dst, scalar=-1.0, in1=mag, op0=ALU.add, op1=ALU.mult)

            ps_row = PS[0:NB, 1:3, :].rearrange("p a (k d) -> p (a k) d", d=D)
            dve.tensor_copy(modrow[:, 0, :], ps_row[:, 0, :])
            dve.tensor_scalar(modrow[:, 1, :], ps_row[:, 1, :], 1.0, None, ALU.add)
            gate(modrow[:, 2, :], ps_row[:, 2, :], rmag[:, 0, :]).then_inc(s["modsb"], 1)
            gate(modrow[:, 3, :], ps_row[:, 5, :], rmag[:, 1, :]).then_inc(s["modsb"], 1)
            ps_T = PS[:, 3, 0:12 * NB].rearrange("p (l k b) -> p l k b", l=2, k=6)
            for k in (0, 3):
                dve.tensor_copy(modT[:, :, k, :], ps_T[:, :, k, :])
                first.did(dve.tensor_scalar(modT[:, :, k + 1, :], ps_T[:, :, k + 1, :], 1.0, None, ALU.add))
                i = gate(modT[:, :, k + 2, :], ps_T[:, :, k + 2, :], gmag[:, :, :])
                if k == 0:
                    first.did(i)
                    first.wait()
                else:
                    i.then_inc(s["modsb"], 1)
            FIRST = first.n

            def rows(k, b):
                return BC[:, b, k, :].unsqueeze(1).broadcast_to([P, NT, D])

            def statistics(src):
                for t in range(NT):
                    dve.bn_stats(stats[:, t, :], src[:, t, :])
                dve.drain()
                for t in range(NT):
                    i = dve.bn_aggr(mv[:, t, :], stats[:, t, :])
                i.then_inc(s["stat"], 1)

            def normalize(src, nth, b):
                dve.wait_ge(s["rstd"], 2 * b + nth)
                dve.wait_ge(s["stat"], 2 * b + nth)
                for t in range(NT):
                    i = dve.tensor_scalar(n_tok[:, t, :], src[:, t, :], mv[:, t, 0:1], rstd[:, t:t + 1],
                                          ALU.subtract, ALU.mult)
                return i

            def start_tokens(b):
                ch.batch(b)
                dve.wait_ge(s["x_in"], 16 * b + 16)
                statistics(xs)

            def tokens(b):
                ch.did(normalize(xs, 1, b))
                ch.wait()
                ch.did(dve.tensor_tensor(h_tok[:, :, :], n_tok[:, :, :], rows(1, b), ALU.mult))
                ch.wait()
                dve.tensor_tensor(h_tok[:, :, :], h_tok[:, :, :], rows(0, b), ALU.add).then_inc(s["htok"], 1)

            def norm_diagonals(b):
                dve.wait_ge(s["rn"], b + 1)
                for t in range(NT):
                    i = dve.tensor_scalar(diag[:, t, :], ident[:, :], rn[:, t:t + 1], None, ALU.mult)
                i.then_inc(s["diag"], 1)

            def products_of_norms(b):
                dve.wait_ge(s["rbc"], b + 1)
                for j in range(NT):
                    i = dve.tensor_scalar(R[:, j, :], rbc[:, :], rn[:, j:j + 1], 1.0 / SIM_EPS, ALU.mult, ALU.min)
                i.then_inc(s["R"], 1)

            def similarities(b, j):
                dve.wait_ge(s["dots"], NT * b + j + 1)
                dve.wait_ge(s["R"], b + 1)
                dve.tensor_tensor(R[:, j, :], dots_bank(j), R[:, j, :], ALU.mult).then_inc(s["sim"], 1)

            def attention_out(b):
                dve.wait_ge(s["E"], NT * b + NT)
                ch.did(dve.reciprocal(rsum[:, :], esum[:, :]))
                dve.wait_ge(s["o_ps"], b + 1)
                ch.wait()
                for t in range(NT):
                    i = dve.scalar_tensor_tensor(out=n_tok[:, t, :], in0=PS[:, 0, t * P:(t + 1) * P],
                                                 scalar=rsum[:, t:t + 1], in1=h_tok[:, t, :], op0=ALU.mult, op1=ALU.add)
                ch.did(i)
                ch.wait()
                ch.did(dve.tensor_tensor(n_tok[:, :, :], n_tok[:, :, :], rows(2, b), ALU.mult))
                ch.wait()
                dve.tensor_tensor(x1[:, :, :], xs[:, :, :], n_tok[:, :, :], ALU.add).then_inc(s["x1"], 1)
                dve.wait_ge(s["x1"], b + 1)
                statistics(x1)
                ch.did(dve.tensor_scalar(X[:, b, :, :], x1[:, :, :], 1.0, None, ALU.mult))

            def second_tokens(b):
                normalize(x1, 2, b).then_inc(s["n2tok"], 1)

            def second_modulation(b):
                dve.wait_ge(s["h2_ps"], b + 1)
                dve.tensor_scalar(h2T[:, :], AUX, modT[:, 0, 4, bass.ds(b, 1)], modT[:, 0, 3, bass.ds(b, 1)], ALU.mult,
                                  ALU.add).then_inc(s["h2T"], 1)

            def split_h2(b):
                dve.wait_ge(s["h2T"], b + 1)
                if not (isinstance(b, int) and b == 0):
                    dve.wait_ge(s["mm1"], NU * b)
                ch.did(dve.tensor_copy(h2h[:, :], h2T[:, :]))
                ch.wait()
                dve.tensor_tensor(h2l[:, :], h2T[:, :], h2h[:, :].bitcast(F32), ALU.subtract).then_inc(s["split"], 1)

            ranks = rank[:, :].unsqueeze(1).broadcast_to([P, NT, NR])
            mo = Chain(dve, s["route_steps"], 1 + 5 + 1 + 5 + 3, FIRST)

            def each(v):
                return v[:, :].unsqueeze(2).broadcast_to([P, NT, NR])

            def first_largest(sel, src, top):
                mo.wait()
                mo.did(dve.tensor_reduce(top[:, :], src[:, :, :], AX_X, ALU.max))
                mo.wait()
                mo.did(dve.tensor_tensor(key[:, :, :], src[:, :, :], each(top), ALU.is_equal))
                mo.wait()
                mo.did(dve.tensor_tensor(key[:, :, :], key[:, :, :], ranks, ALU.mult))
                mo.wait()
                mo.did(dve.tensor_reduce(r1[:, :], key[:, :, :], AX_X, ALU.max))
                mo.wait()
                mo.did(dve.tensor_tensor(sel[:, :, :], ranks, each(r1), ALU.is_equal))

            def route_first(b):
                mo.batch(b)
                dve.wait_ge(s["logit_ps"], b + 1)
                mo.did(dve.tensor_tensor(L[:, :, :], PS[:, 1, 0:NT * NR].rearrange("p (t e) -> p t e", t=NT),
                                         rb[:, :].unsqueeze(1).broadcast_to([P, NT, NR]), ALU.add))
                first_largest(sel1, L, m1)

            def route_second(b):
                mo.wait()
                mo.did(dve.scalar_tensor_tensor(out=Lb[:, :, :], in0=sel1[:, :, :], scalar=-BIG, in1=L[:, :, :],
                                                op0=ALU.mult, op1=ALU.add))
                first_largest(sel2, Lb, m2)
                mo.wait()
                dve.tensor_tensor(dm[:, :], m1[:, :], m2[:, :], ALU.subtract).then_inc(s["top"], 1)

            def route_weights(b):
                dve.wait_ge(s["th"], b + 1)
                dve.tensor_scalar(w1st[:, :], th[:, :], 0.5, 0.5, ALU.mult, ALU.add)
                mo.did(dve.tensor_scalar(w2nd[:, :], th[:, :], -0.5, 0.5, ALU.mult, ALU.add))
                mo.wait()
                mo.did(dve.tensor_tensor(sel1[:, :, :], sel1[:, :, :], each(w1st), ALU.mult))
                mo.did(dve.tensor_tensor(sel2[:, :, :], sel2[:, :, :], each(w2nd), ALU.mult))
                mo.wait()
                dve.tensor_tensor(comb[:, :, :], sel1[:, :, :], sel2[:, :, :], ALU.add).then_inc(s["comb"], 1)

            def split_chunk(b, i):
                if i % NC not in VCH:
                    return
                dve.wait_ge(s["g"], NU * b + i + 1)
                if not (isinstance(b, int) and b == 0 and i < RING):
                    dve.wait_ge(s["mm2"], NU * b + i - RING + 1)
                dve.tensor_copy(gh[:, i % RING, :], g[:, i % RING, :]).then_inc(s["ghv"], 1)
                dve.wait_ge(s["ghv"], NE * len(VCH) * b + len(VCH) * (i // NC) + VCH.index(i % NC) + 1)
                dve.tensor_tensor(gl[:, i % RING, :], g[:, i % RING, :], gh[:, i % RING, :].bitcast(F32),
                                  ALU.subtract).then_inc(s["glv"], 1)

            def expert_out(b, e):
                dve.wait_ge(s["mm2"], NU * b + NC * (e + 1))
                if e == 0:
                    if not (isinstance(b, int) and b == 0):
                        dve.wait_ge(s["z_ps"], b)
                    dve.tensor_scalar(acc[:, :], y_bank(e), b2[:, 0:1], None, ALU.add).then_inc(s["y_used"], 1)
                    return
                dve.wait_ge(s["wb1"] if e <= 2 else s["wb2"], 16 * b + 16)
                if e >= 3:
                    dve.wait_ge(s["acc"], NR * b + e - 2)
                dve.scalar_tensor_tensor(out=tmp[:, e % 2, :], in0=y_bank(e), scalar=b2[:, e:e + 1],
                                         in1=WB[:, e - 1, :], op0=ALU.add, op1=ALU.mult).then_inc(s["y_used"], 1)
                if e >= 2:
                    add_expert(b, e - 1)
                if e == NE - 1:
                    add_expert(b, e)

            def add_expert(b, e):
                dve.wait_ge(s["y_used"], NE * b + e + 1)
                if e >= 2:
                    dve.wait_ge(s["acc"], NR * b + e - 1)
                dve.tensor_tensor(acc[:, :], acc[:, :], tmp[:, e % 2, :], ALU.add).then_inc(s["acc"], 1)

            def finish(b):
                dve.wait_ge(s["z_ps"], b + 1)
                dve.tensor_tensor(z_tok[:, :, :], PS[:, 2, :].rearrange("p (t d) -> p t d", t=NT), rows(3, b),
                                  ALU.mult).then_inc(s["z_used"], 1)
                dve.wait_ge(s["z_used"], b + 1)
                dve.tensor_tensor(X[:, b, :, :], X[:, b, :, :], z_tok[:, :, :], ALU.add)

            def low_weights(e0, e1):
                for e in range(e0, e1):
                    dve.wait_ge(s["whi"], 2 * e + 2)
                    dve.tensor_tensor(w2l[:, e, :, :].rearrange("p c d -> p (c d)"), stage[:, e % STAGES, 1, :],
                                      w2h[:, e, :, :].rearrange("p c d -> p (c d)").bitcast(F32),
                                      ALU.subtract).then_inc(s["wlo2"], 1)

            start_tokens(0)
            low_weights(0, 2)
            dve.wait_ge(s["bc0"], 16)
            tokens(0)
            low_weights(2, 4)
            norm_diagonals(0)
            products_of_norms(0)
            for j in range(NT):
                similarities(0, j)
            low_weights(4, 6)
            attention_out(0)
            second_tokens(0)
            second_modulation(0)
            split_h2(0)
            low_weights(6, NE)
            dve.wait_ge(s["bc"], 16)

            def pair(b, before=True, after=True):
                for i in range(NU):
                    split_chunk(b, i)
                    if i == V_ROUTE1:
                        route_first(b)
                    if i == V_ROUTE2:
                        route_second(b)
                    if i == V_ROUTE3:
                        route_weights(b)
                    if before and i == V_Z:
                        finish(b - 1)
                    if after:
                        if i == V_START:
                            start_tokens(b + 1)
                        if i == V_TOK:
                            tokens(b + 1)
                        if i == V_DIAG:
                            norm_diagonals(b + 1)
                        if i == V_R:
                            products_of_norms(b + 1)
                        if V_SIM <= i < V_SIM + NT:
                            similarities(b + 1, i - V_SIM)
                        if i == V_OUT:
                            attention_out(b + 1)
                        if i == V_TOK2:
                            second_tokens(b + 1)
                        if i == V_MOD:
                            second_modulation(b + 1)
                    if i >= Y_AT and (i - Y_AT) % NC == 0:
                        expert_out(b, (i - Y_AT) // NC)
                for e in range((NU - 1 - Y_AT) // NC + 1, NE - 1):
                    expert_out(b, e)
                if after:
                    split_h2(b + 1)
                expert_out(b, NE - 1)

            pair(0, before=False)
            with dve.Fori(1, NB - 1) as b:
                pair(b)
            pair(NB - 1, after=False)
            finish(NB - 1)


def layer1(nc, out, X, modT, eye, maskf, wq, wout, gw, gbias, dram):
    q_d, k_d = dram("q_d", [NPART, HD, NH, S], BF16), dram("k_d", [NPART, NPART, HD, NH, S], BF16)
    mx_d, o_d = dram("mx_d", [NPART, NH * S], BF16), dram("o_d", [2, P, S])
    with ExitStack() as ctx:
        def sb(name, shape, dt=F32):
            return ctx.enter_context(nc.sbuf_tensor(name, shape, dt))

        def sem(name):
            return ctx.enter_context(nc.semaphore("b_" + name))

        one = sb("one", [P, 1])
        eye16, mask16, maskT16 = sb("eye16", [P, P], BF16), sb("mask16", [P, P], BF16), sb("maskT16", [P, P], BF16)
        ones16 = sb("ones16", [NPART, S], BF16)
        wsum, yscale = sb("free wsum", [P, 1]), sb("yscale", [P, NB])
        gbh = sb("gbh", [P, 2])
        half, eps = sb("halfb", [P, NT]), sb("epsb", [P, NT])
        stat3, mv3, rstd3 = sb("stat3", [P, NT, 6]), sb("mv3", [P, NT, 2]), sb("rstd3", [P, NT])
        n3 = sb("n3", [P, NT, D])
        h3 = sb("h3", [P, S])
        qf, kf, qleft, kleft = sb("qf", [P, S]), sb("kf", [P, S]), sb("qleft", [P, S]), sb("kleft", [P, S])
        q3, k3 = sb("q3", [P, NPART, S], BF16), sb("k3", [P, NPART, S], BF16)
        QST, KST = sb("QST", [KMAX, 2, NH, S], BF16), sb("KST", [KMAX, 2, NH, S], BF16)
        VA = sb("VA", [P, 2, NT, NH, VW])
        nm = sb("nm", [P, 2, NH, NT])
        nmT, nleft = sb("nmT", [NH * NT, P]), sb("nleft", [NH * NT, P])
        nm3 = sb("nm3", [NH * NT, NPART, P], BF16)
        W = sb("W", [P, 2, UG, S])
        OT = sb("OT", [P, 2, S])
        Z, rz, zT = sb("Z", [P, HD + 1, S // HD]), sb("rz", [P, S // HD]), sb("zT", [P, S])
        stat4, mv4, rstd4 = sb("stat4", [P, NT, 6]), sb("mv4", [P, NT, 2]), sb("rstd4", [P, NT])
        n4 = sb("n4", [P, NT, D])
        h4 = sb("h4", [P, S])
        gates, cst = sb("gates", [P, 3, S]), sb("cst", [P, S])
        keep, new = sb("keep", [P, S]), sb("new", [P, S])
        XO = sb("XO", [P, NB, S])
        cu = qleft
        PS = ctx.enter_context(nc.psum_tensor("PB", [P, 8, S], F32))
        AUX = PS[:, 0, :]
        OUT = (6, 7)
        ROW = (1, 2, OUT[1])

        GATES = (C_G0, C_G1, C_G2, C_G3)
        names = ("free wsum const eyes gbh zero onesrow st3 rs3 n3 h3_ps h3 q_ps qf k_ps kf ql kl q1 k1 q3 k3"
                 " qd kd qst0 qst1 v_ps va sc mx nm_ps nmT nm3 mxd mxs sT w pv po0 po1 od0 od1 z zT x3_ps x3 st4"
                 " rs4 n4 h4_ps h4 g_ps gate xo c cu_ps cu pre th hg f_ps fin store root3_steps root4_steps"
                 " split_steps state_steps").split()
        s = {n: sem(n) for n in names}
        block = ctx.enter_context(nc.Block())

        def bodies(eng, body):
            body(0, 0, False, True, True)
            with eng.Fori(0, (NB - 4) // 2) as r:
                for k in range(2):
                    body(2 * r + k + 1, (k + 1) % 2, True, True, True)
            body(NB - 3, (NB - 3) % 2, True, True, True)
            body(NB - 2, (NB - 2) % 2, True, True, False)
            body(NB - 1, (NB - 1) % 2, True, False, False)

        @block.sync
        def _(sp):
            sp.wait_ge(s["const"], 1)
            for par in range(2):
                sp.dma_start(KST[KROWS:KMAX, par, :, :],
                             ones16[:, :].unsqueeze(1).broadcast_to([NPART, NH, S])).then_inc(s["onesrow"], 16)

            def keep_parts(b):
                sp.wait_ge(s["q3"], b + 1)
                sp.dma_start(q_d.rearrange("s h n q -> (h n) s q"), q3[:, :, :]).then_inc(s["qd"], 16)
                sp.wait_ge(s["k3"], b + 1)
                for sq in range(NPART):
                    sp.dma_start(k_d[:, sq].rearrange("s h n q -> (h n) s q"), k3[:, :, :]).then_inc(s["kd"], 16)

            def stack(b, par, part):
                heads = slice(part * NH // 2, (part + 1) * NH // 2)
                if not (isinstance(b, int) and b < 2):
                    sp.wait_ge(s["sT"], NV * (b - 2) + NV // 2 * (part + 1))
                    sp.sem_inc(s["free"], 1)
                sp.wait_ge(s["qd"], 16 * b + 16)
                for sk in range(NPART):
                    sp.dma_start(QST[sk * NPART * HD:(sk + 1) * NPART * HD, par, heads, :],
                                 q_d[:, :, heads, :].rearrange("s h n q -> (s h) n q")).then_inc(s[f"qst{part}"], 16)
                sp.wait_ge(s["kd"], 48 * b + 48)
                sp.dma_start(KST[0:KROWS, par, heads, :],
                             k_d[:, :, :, heads, :].rearrange("k s h n q -> (k s h) n q")).then_inc(s[f"qst{part}"], 16)

            def share_maxima(b, par):
                sp.wait_ge(s["nm3"], b + 1)
                sp.dma_start(mx_d.rearrange("s (k q) -> k s q", q=P), nm3[:, :, :]).then_inc(s["mxd"], 16)
                sp.wait_ge(s["mxd"], 16 * b + 16)
                sp.dma_start(QST[KROWS:KMAX, par, :, :].rearrange("p n q -> p (n q)"), mx_d).then_inc(s["mxs"], 16)

            def keep_out(b, bank):
                sp.wait_ge(s[f"po{bank}"], b + 1)
                sp.dma_start(o_d[bank], OT[:, bank, :]).then_inc(s[f"od{bank}"], 16)

            def reshape_out(b, bank):
                sp.wait_ge(s[f"od{bank}"], 16 * b + 16)
                for n in (range(0, 12), range(12, NH))[bank]:
                    row = 32 * (n % 4) + (n // 4 % 3) * (HD + 1)
                    sp.dma_start(Z[n * HD:(n + 1) * HD, :, :],
                                 o_d[bank, row:row + HD + 1, :].rearrange("c (a r) -> a c r", a=HD)).then_inc(s["z"], 16)

            for b in range(2):
                keep_parts(b)
                if b == 1:
                    sp.wait_ge(s["sc"], NM // 2 + 1)
                for part in range(2):
                    stack(b, b, part)
            share_maxima(0, 0)

            def body(b, par, before, after, ahead):
                if ahead:
                    keep_parts(b + 2)
                    stack(b + 2, par, 0)
                keep_out(b, 0)
                if after:
                    share_maxima(b + 1, 1 - par)
                reshape_out(b, 0)
                if ahead:
                    stack(b + 2, par, 1)
                keep_out(b, 1)
                reshape_out(b, 1)

            bodies(sp, body)
            for b in range(NB):
                sp.wait_ge(s["fin"], b + 1)
                sp.dma_start(out[b].rearrange("(t p) d -> p t d", p=P), X[:, b, :, :]).then_inc(s["store"], 16)
            sp.wait_ge(s["store"], 16 * NB)

        @block.gpsimd
        def _(pool):
            pool.memset(half[:, :], -0.5)
            pool.memset(eps[:, :], LN_EPS)
            pool.memset(one[:, :], 1.0)
            pool.memset(nm[:, :, :, :], 0.0)
            pool.memset(ones16[:, :], 1.0).then_inc(s["const"], 1)
            ch = Chain(pool, s["root3_steps"], 1)
            ch4 = Chain(pool, s["root4_steps"], 1)

            def inverse_root(ch, dst, src, ready):
                ch.did(pool.tensor_tensor(dst, src, eps[:, :], ALU.add))
                ch.wait()
                pool.tensor_tensor(dst, dst, half[:, :], ALU.pow).then_inc(ready, 1)

            def rstd_third(b):
                ch.batch(b)
                pool.wait_ge(s["st3"], b + 1)
                inverse_root(ch, rstd3[:, :], mv3[:, :, 1], s["rs3"])

            def leave(b):
                for src, parts, left, come, ready in ((qf, q3, qleft, "qf", "ql"), (kf, k3, kleft, "kf", "kl")):
                    pool.wait_ge(s[come], b + 1)
                    pool.tensor_tensor(left[:, :], src[:, :], parts[:, 0, :], ALU.subtract).then_inc(s[ready], 1)
                for parts, left, come, ready in ((q3, qleft, "q1", "q3"), (k3, kleft, "k1", "k3")):
                    pool.wait_ge(s[come], b + 1)
                    pool.tensor_tensor(parts[:, 2, :], left[:, :], parts[:, 1, :], ALU.subtract).then_inc(s[ready], 1)

            def rstd_fourth(b):
                ch4.batch(b)
                pool.wait_ge(s["st4"], b + 1)
                inverse_root(ch4, rstd4[:, :], mv4[:, :, 1], s["rs4"])

            pool.wait_ge(s["const"], 1)
            rstd_third(0)
            pool.memset(VA[:, :, :, :, :], 0.0).then_inc(s["zero"], 1)
            pool.wait_ge(s["zero"], 1)
            for j in range(4):
                c = (j % 3) * (HD + 1) + HD
                i = pool.memset(VA[:, :, :, 4 * j:4 * j + 4, c:c + 1].rearrange("p a k n o -> p (a k) (n o)"), 1.0)
            i.then_inc(s["zero"], 1)
            leave(0)
            rstd_third(1)
            leave(1)

            def body(b, par, before, after, ahead):
                if ahead:
                    rstd_third(b + 2)
                    leave(b + 2)
                if before:
                    rstd_fourth(b - 1)

            bodies(pool, body)
            rstd_fourth(NB - 1)

        @block.scalar
        def _(act):
            def project_q(b):
                act.wait_ge(s["q_ps"], b + 1)
                act.activation(qf[:, :], AUX, ACT.Copy, scale=float(HD) ** -0.5)
                if not (isinstance(b, int) and b == 0):
                    act.wait_ge(s["qst1"], 64 * b)
                act.activation(q3[:, 0, :], AUX, ACT.Copy, scale=float(HD) ** -0.5).then_inc(s["qf"], 1)

            def project_k(b):
                act.wait_ge(s["k_ps"], b + 1)
                act.copy(kf[:, :], AUX)
                act.copy(k3[:, 0, :], AUX).then_inc(s["kf"], 1)

            def second_q(b):
                act.wait_ge(s["ql"], b + 1)
                act.copy(q3[:, 1, :], qleft[:, :]).then_inc(s["q1"], 1)

            def second_k(b):
                act.wait_ge(s["kl"], b + 1)
                act.copy(k3[:, 1, :], kleft[:, :]).then_inc(s["k1"], 1)

            def place_values(b, par):
                act.wait_ge(s["v_ps"], b + 1)
                v_ps = AUX.rearrange("p (k n h) -> p k n h", k=NT, h=HD)
                for j in range(4):
                    c = (j % 3) * (HD + 1)
                    i = act.copy(VA[:, par, :, 4 * j:4 * j + 4, c:c + HD], v_ps[:, :, 4 * j:4 * j + 4, :])
                i.then_inc(s["va"], 1)

            def modulate(b, dst, k, come, ready):
                act.wait_ge(come, b + 1)
                act.activation(dst[:, :], AUX, ACT.Identity, scale=modT[:, 1, k + 1, bass.ds(b, 1)],
                               bias=modT[:, 1, k, bass.ds(b, 1)]).then_inc(ready, 1)

            def exps(b, v):
                j = v // UG
                act.wait_ge(s["sT"], NV * b + v + 1)
                if v % UG == 0 and not (isinstance(b, int) and b == 0 and j < 2):
                    act.wait_ge(s["pv"], 4 * b + j - 1)
                act.activation(W[:, j % 2, v % UG, :], PS[:, 3 + v % 3, :], ACT.Exp).then_inc(s["w"], 1)

            def copy_out(b, bank):
                act.wait_ge(s["pv"], 4 * b + 3 + bank)
                act.copy(OT[:, bank, :], PS[:, OUT[bank], :]).then_inc(s[f"po{bank}"], 1)

            def gate(b, k, bank=AUX):
                act.wait_ge(s["g_ps"], 4 * b + k + 1)
                if k == 3:
                    act.activation(XO[:, b, :], bank, ACT.Identity, bias=gbias[:, 3:4]).then_inc(s["xo"], 1)
                    return
                act.activation(gates[:, k, :], bank, ACT.Tanh, bias=gbh[:, k:k + 1] if k < 2 else gbias[:, 2:3],
                               scale=0.5 if k < 2 else 1.0).then_inc(s["gate"], 1)

            act.wait_ge(s["gbh"], 1)
            modulate(0, h3, 0, s["h3_ps"], s["h3"])
            project_q(0)
            project_k(0)
            act.wait_ge(s["zero"], 2)
            place_values(0, 0)
            second_q(0)
            second_k(0)
            modulate(1, h3, 0, s["h3_ps"], s["h3"])
            project_q(1)
            project_k(1)
            second_q(1)
            second_k(1)

            def body(b, par, before, after, ahead):
                for v in range(NV):
                    exps(b, v)
                    if after and v == C_V:
                        place_values(b + 1, 1 - par)
                    if ahead and v == C_H3:
                        modulate(b + 2, h3, 0, s["h3_ps"], s["h3"])
                    if ahead and v == C_Q:
                        project_q(b + 2)
                    if ahead and v == C_K:
                        project_k(b + 2)
                    if ahead and v == C_Q + C_PART:
                        second_q(b + 2)
                    if ahead and v == C_K + C_PART:
                        second_k(b + 2)
                    if before and v == C_H4:
                        modulate(b - 1, h4, 3, s["h4_ps"], s["h4"])
                    if before and v in GATES:
                        gate(b - 1, GATES.index(v))
                    if v == C_OUT:
                        copy_out(b, 0)
                copy_out(b, 1)

            bodies(act, body)
            modulate(NB - 1, h4, 3, s["h4_ps"], s["h4"])
            for k in range(4):
                gate(NB - 1, k, PS[:, k, :])
            act.wait_ge(s["cu_ps"], 1)
            act.copy(cu[:, :], PS[:, 4, :]).then_inc(s["cu"], 1)
            for b in range(NB):
                act.wait_ge(s["pre"], b + 1)
                act.activation(W[:, 0, b, :], W[:, 0, b, :], ACT.Tanh).then_inc(s["th"], 1)

        @block.tensor
        def _(pe):

            def tiles(v):
                return v[:, :].rearrange("p (t q) -> p t q", t=NT)

            def transposes(bank, src, ready):
                for t in range(NT):
                    i = pe.transpose(bank[:, t * P:(t + 1) * P], src[:, t, :], eye[:, :])
                i.then_inc(ready, 1)

            def transpose_third(b):
                pe.wait_ge(s["n3"], b + 1)
                if not (isinstance(b, int) and b == 0):
                    pe.wait_ge(s["va"], b)
                transposes(AUX, n3, s["h3_ps"])

            def project_q(b):
                pe.wait_ge(s["h3"], b + 1)
                pe.matmul(AUX, wq[:, 0, :], h3[:, :], start=True, stop=True).then_inc(s["q_ps"], 1)

            def project_k(b):
                pe.wait_ge(s["qf"], b + 1)
                pe.matmul(AUX, wq[:, 1, :], h3[:, :], start=True, stop=True).then_inc(s["k_ps"], 1)

            def project_v(b):
                if isinstance(b, int) and b == 0:
                    pe.wait_ge(s["kf"], 1)
                else:
                    pe.wait_ge(s["nmT"], b)
                for t in range(NT):
                    i = pe.matmul(AUX[:, t * P:(t + 1) * P], h3[:, t * P:(t + 1) * P], wq[:, 2, :], start=True, stop=True)
                i.then_inc(s["v_ps"], 1)

            def row_scores(b, par, u):
                g4, (t, heads) = u // len(MAX_UNITS), MAX_UNITS[u % len(MAX_UNITS)]
                if u == 0:
                    pe.wait_ge(s["qst0"], 64 * b + 64)
                if u == NM // 2:
                    pe.wait_ge(s["qst1"], 64 * b + 64)
                if u >= 3:
                    pe.wait_ge(s["mx"], NM * b + u - 2)
                if u == 2 and not (isinstance(b, int) and b < 2):
                    pe.wait_ge(s["po1"], b - 1)
                cols = (t + 1) * P
                for i, n in enumerate(heads):
                    n += 4 * g4
                    c0 = i * cols
                    bank = PS[:, ROW[u % 3], :]
                    pe.matmul(bank[:, c0:c0 + cols], QST[0:KROWS, par, n, t * P:(t + 1) * P], KST[0:KROWS, par, n, 0:cols],
                              start=True, stop=False)
                    last = pe.matmul(bank[:, c0 + t * P:c0 + cols], eye16[:, :], mask16[:, :], start=False, stop=True)
                last.then_inc(s["sc"], 1)

            def transpose_maxima(b):
                pe.wait_ge(s["mx"], NM * b + NM)
                pe.transpose(PS[:, 0, 0:P], nm[:, :, :, :].rearrange("p a n t -> p (a n t)"), eye[:, :]).then_inc(s["nm_ps"], 1)

            def scores(b, par, v):
                if v == 0:
                    pe.wait_ge(s["mxs"], 16 * b + 16)
                    if not (isinstance(b, int) and b == 0):
                        pe.wait_ge(s["w"], NV * b)
                elif v >= 3:
                    pe.wait_ge(s["w"], NV * b + v - 2)
                for n, k, c0 in UNITS[v % UG]:
                    n += 4 * (v // UG)
                    bank, cols = PS[:, 3 + v % 3, :], (NT - k) * P
                    pe.matmul(bank[:, c0:c0 + cols], KST[:, par, n, k * P:(k + 1) * P], QST[:, par, n, k * P:S],
                              start=True, stop=False)
                    last = pe.matmul(bank[:, c0:c0 + P], eye16[:, :], maskT16[:, :], start=False, stop=True)
                last.then_inc(s["sT"], 1)

            def values(b, par, j):
                pe.wait_ge(s["w"], NV * b + UG * (j + 1))
                if j == 3 and not (isinstance(b, int) and b == NB - 1):
                    pe.wait_ge(s["mx"], NM * b + 2 * NM)
                if j in (0, 3) and not (isinstance(b, int) and b == 0):
                    pe.wait_ge(s[f"po{j // 3}"], b)
                if j == 0:
                    pe.wait_ge(s["va"], b + 1)
                for k in range(NT):
                    for quad in range(4):
                        u, c0 = WHERE[quad, k]
                        last = pe.matmul(PS[32 * quad:32 * quad + 32, OUT[j // 3], k * P:S], VA[:, par, k, 4 * j + quad, :],
                                         W[:, j % 2, u, c0:c0 + (NT - k) * P], start=(k == 0 and j in (0, 3)),
                                         stop=(k == NT - 1 and j >= 2))
                last.then_inc(s["pv"], 1)

            def transpose_out(b):
                pe.wait_ge(s["zT"], b + 1)
                transposes(AUX, tiles(zT), s["x3_ps"])

            def transpose_fourth(b):
                pe.wait_ge(s["n4"], b + 1)
                transposes(AUX, n4, s["h4_ps"])

            def gate_sums(b, k, bank=AUX):
                if k == 0:
                    pe.wait_ge(s["h4"], b + 1)
                    pe.wait_ge(s["c"], b + 1)
                elif bank is AUX:
                    pe.wait_ge(s["gate"], 3 * b + k)
                i = pe.matmul(bank, gw[:, 2 * k, :], h4[:, :], start=True, stop=(k == 3))
                if k < 3:
                    i = pe.matmul(bank, gw[:, 2 * k + 1, :], cst[:, :], start=False, stop=True)
                i.then_inc(s["g_ps"], 1)

            transpose_third(0)
            project_q(0)
            project_k(0)
            project_v(0)
            pe.wait_ge(s["const"], 1)
            pe.matmul(PS[:, 1, 0:1], wout[:, :], one[:, :], start=True, stop=True).then_inc(s["wsum"], 1)
            transpose_third(1)
            project_q(1)
            project_k(1)
            pe.wait_ge(s["eyes"], 1)
            pe.wait_ge(s["onesrow"], 32)
            for u in range(NM):
                row_scores(0, 0, u)
            pe.wait_ge(s["kf"], 2)
            transpose_maxima(0)

            def body(b, par, before, after, ahead):
                for v in range(NV):
                    scores(b, par, v)
                    if v >= UG and (v - C_LAG) % UG == UG - 1:
                        values(b, par, (v - C_LAG) // UG)
                    if after and v == C_V:
                        project_v(b + 1)
                    if ahead and v == C_H3:
                        transpose_third(b + 2)
                    if ahead and v == C_Q:
                        project_q(b + 2)
                    if ahead and v == C_K:
                        project_k(b + 2)
                    if before and v == C_X3:
                        pe.wait_ge(s["kf"], b + 3) if ahead else pe.wait_ge(s["va"], NB)
                        transpose_out(b - 1)
                    if before and v == C_H4:
                        transpose_fourth(b - 1)
                    if before and v in GATES:
                        gate_sums(b - 1, GATES.index(v))
                    if after:
                        for u in range(issued(v - 1), issued(v)):
                            row_scores(b + 1, 1 - par, u)
                    if after and v == C_NM:
                        pe.wait_ge(s["xo"], b) if before else pe.wait_ge(s["kf"], 3)
                        transpose_maxima(b + 1)
                values(b, par, 3)

            bodies(pe, body)
            transpose_out(NB - 1)
            transpose_fourth(NB - 1)
            for k in range(4):
                gate_sums(NB - 1, k, PS[:, k, :])
            pe.wait_ge(s["c"], NB + 1)
            pe.matmul(PS[:, 4, :], gw[:, 7, :], cst[:, :], start=True, stop=True).then_inc(s["cu_ps"], 1)
            for b in range(NB):
                if b == 4:
                    pe.wait_ge(s["cu"], 1)
                pe.wait_ge(s["hg"], b + 1)
                transposes(PS[:, b, :], W[:, 0, b, :].rearrange("p (t q) -> p t q", t=NT), s["f_ps"])

        @block.vector
        def _(dve):
            mx = Chain(dve, s["split_steps"], 3)
            rec = Chain(dve, s["state_steps"], 3)

            def statistics(b, stats, mv, ready):
                for t in range(NT):
                    dve.bn_stats(stats[:, t, :], X[:, b, t, :])
                dve.drain()
                for t in range(NT):
                    i = dve.bn_aggr(mv[:, t, :], stats[:, t, :])
                i.then_inc(ready, 1)

            def normalize(b, dst, mv, rstd, ready):
                for t in range(NT):
                    i = dve.tensor_scalar(dst[:, t, :], X[:, b, t, :], mv[:, t, 0:1], rstd[:, t:t + 1],
                                          ALU.subtract, ALU.mult)
                i.then_inc(ready, 1)

            def split(ch, parts, src, left, ready):
                ch.did(dve.tensor_copy(parts[:, 0, :], src))
                ch.wait()
                ch.did(dve.tensor_tensor(left, src, parts[:, 0, :], ALU.subtract))
                ch.wait()
                ch.did(dve.tensor_copy(parts[:, 1, :], left))
                ch.wait()
                dve.tensor_tensor(parts[:, 2, :], left, parts[:, 1, :], ALU.subtract).then_inc(ready, 1)

            def normalize_third(b):
                dve.wait_ge(s["rs3"], b + 1)
                dve.wait_ge(s["st3"], b + 1)
                normalize(b, n3, mv3, rstd3, s["n3"])

            def maxima(b, u):
                g4, (t, heads) = u // len(MAX_UNITS), MAX_UNITS[u % len(MAX_UNITS)]
                dve.wait_ge(s["sc"], NM * b + u + 1)
                n0, k, cols = 4 * g4 + heads[0], len(heads), (t + 1) * P
                dve.tensor_reduce(nm[:, 0, n0:n0 + k, t], PS[:, ROW[u % 3], 0:k * cols].rearrange("p (k q) -> p k q", k=k),
                                  AX_X, ALU.max, negate=True).then_inc(s["mx"], 1)

            def split_maxima(b):
                dve.wait_ge(s["nm_ps"], b + 1)
                dve.tensor_copy(nmT[:, :], PS[0:NH * NT, 0, 0:P]).then_inc(s["nmT"], 1)
                mx.batch(b)
                dve.wait_ge(s["nmT"], b + 1)
                split(mx, nm3, nmT[:, :], nleft[:, :], s["nm3"])

            def scale_out(b):
                dve.wait_ge(s["z"], 16 * NH * b + 16 * NH)
                dve.reciprocal(rz[:, :], Z[:, HD, :])
                dve.drain()
                dve.scalar_tensor_tensor(out=zT[:, :].rearrange("p (r h) -> p h r", h=HD), in0=Z[:, 0:HD, :],
                                         scalar=yscale[:, bass.ds(b, 1)],
                                         in1=rz[:, :].unsqueeze(1).broadcast_to([P, HD, S // HD]),
                                         op0=ALU.mult, op1=ALU.mult).then_inc(s["zT"], 1)

            def add_attention(b):
                dve.wait_ge(s["x3_ps"], b + 1)
                dve.tensor_tensor(X[:, b, :, :], X[:, b, :, :], AUX.rearrange("p (t d) -> p t d", t=NT),
                                  ALU.add).then_inc(s["x3"], 1)
                dve.drain()
                statistics(b, stat4, mv4, s["st4"])

            def normalize_fourth(b):
                dve.wait_ge(s["rs4"], b + 1)
                dve.wait_ge(s["st4"], b + 1)
                normalize(b, n4, mv4, rstd4, s["n4"])

            def recur(b):
                rec.batch(b)
                dve.wait_ge(s["gate"], 3 * b + 3)
                dve.wait_ge(s["g_ps"], 4 * b + 3)
                rec.did(dve.scalar_tensor_tensor(out=keep[:, :], in0=gates[:, 0, :], scalar=1.0, in1=cst[:, :], op0=ALU.add, op1=ALU.mult))
                rec.did(dve.scalar_tensor_tensor(out=new[:, :], in0=gates[:, 1, :], scalar=1.0, in1=gates[:, 2, :], op0=ALU.add, op1=ALU.mult))
                rec.wait()
                rec.did(dve.tensor_tensor(keep[:, :], keep[:, :], new[:, :], ALU.add))
                rec.wait()
                dve.tensor_scalar(cst[:, :], keep[:, :], 0.5, None, ALU.mult).then_inc(s["c"], 1)

            def met(v):
                return min(issued(v) - 1 + D_GAP, NM - 1)

            statistics(0, stat3, mv3, s["st3"])
            dve.memset(cst[:, :], 0.0)
            dve.tensor_scalar(gbh[:, :], gbias[:, 0:2], 0.5, None, ALU.mult).then_inc(s["gbh"], 1)
            normalize_third(0)
            dve.tensor_copy(eye16[:, :], eye[:, :])
            dve.tensor_copy(mask16[:, :], maskf[:, 0, :])
            dve.tensor_copy(maskT16[:, :], maskf[:, 1, :]).then_inc(s["eyes"], 1)
            dve.wait_ge(s["wsum"], 1)
            dve.tensor_copy(wsum[:, :], PS[:, 1, 0:1])
            dve.drain()
            dve.tensor_scalar(yscale[:, :], modT[:, 1, 2, :], wsum[:, 0:1], None, ALU.mult)
            dve.tensor_scalar(cst[:, :], cst[:, :], gbias[:, 4:5], None, ALU.add).then_inc(s["c"], 1)
            statistics(1, stat3, mv3, s["st3"])
            normalize_third(1)
            for u in range(NM):
                maxima(0, u)
            split_maxima(0)

            def body(b, par, before, after, ahead):
                if ahead:
                    statistics(b + 2, stat3, mv3, s["st3"])
                    normalize_third(b + 2)
                for u in range(NM):
                    if after:
                        maxima(b + 1, u)
                    if before and u == D_Z:
                        scale_out(b - 1)
                    if before and u == met(C_X3):
                        add_attention(b - 1)
                    if before and u == D_N4:
                        normalize_fourth(b - 1)
                    if before and u == met(C_G2):
                        recur(b - 1)
                if after:
                    split_maxima(b + 1)

            bodies(dve, body)
            scale_out(NB - 1)
            add_attention(NB - 1)
            normalize_fourth(NB - 1)
            recur(NB - 1)
            dve.wait_ge(s["cu"], 1)
            dve.wait_ge(s["xo"], NB)
            for b in range(NB):
                dve.tensor_tensor(W[:, 0, b, :], XO[:, b, :], cu[:, :], ALU.add).then_inc(s["pre"], 1)
            for b in range(NB):
                dve.wait_ge(s["th"], b + 1)
                dve.tensor_scalar(W[:, 0, b, :], W[:, 0, b, :], modT[:, 1, 5, b:b + 1], None, ALU.mult).then_inc(s["hg"], 1)
            for b in range(NB):
                dve.wait_ge(s["f_ps"], b + 1)
                dve.tensor_tensor(X[:, b, :, :], X[:, b, :, :], PS[:, b, :].rearrange("p (t d) -> p t d", t=NT),
                                  ALU.add).then_inc(s["fin"], 1)


def build(nc, ins, out):
    with ExitStack() as ctx:
        X = ctx.enter_context(nc.sbuf_tensor("X", [P, NB, NT, D], F32))
        modT = ctx.enter_context(nc.sbuf_tensor("modT", [P, 2, 6, NB], F32))

        def dram(name, shape, dt=F32):
            return nc.dram_tensor(name, shape, dt, kind="Internal").ap()

        def sb(name, shape):
            return ctx.enter_context(nc.sbuf_tensor(name, shape, F32))

        ident, maskf, wq, wout = sb("ident", [P, P]), sb("maskf", [P, 2, P]), sb("wq", [P, 3, D]), sb("wout", [P, D])
        gw, gbias = sb("gw", [P, 8, D]), sb("gbias", [P, 5])
        later = [(maskf[:, :, :], ins["mask"]), (wq[:, :, :], ins["wq"]), (wout[:, :], ins["wout"]),
                 (gw[:, :, :], ins["gw"]), (gbias[:, :], ins["gbias"])]
        layer0(nc, ins, X, modT, ident, later, dram)
        layer1(nc, out, X, modT, ident, maskf, wq, wout, gw, gbias, dram)


def host_layout(v):
    a = {k: np.asarray(x) for k, x in v.items()}
    w1 = np.concatenate([a["L0_ffn_shared_w1"][None], a["L0_ffn_spec_w1"]])
    w2 = np.concatenate([a["L0_ffn_shared_w2"][None], a["L0_ffn_spec_w2"]])
    b1 = np.concatenate([a["L0_ffn_shared_b1"][None], a["L0_ffn_spec_b1"]])
    b2 = np.concatenate([a["L0_ffn_shared_b2"][None], a["L0_ffn_spec_b2"]])
    wqkv = a["L1_attn_W_qkv"].reshape(NH, D, 3, HD)
    return {
        "x": a["L0_attn_x"],
        "cT": np.stack([a["L0_c"].T, a["L1_c"].T], 1),
        "wmod": np.stack([a["L0_wmod"], a["L1_wmod"]], 1).reshape(D, 2, 6, D),
        "w1": w1.transpose(2, 0, 1),
        "w2": w2.reshape(NE, D, NC, P).transpose(3, 0, 2, 1),
        "b1": b1.reshape(NE, NC, P).transpose(2, 0, 1),
        "b2": b2.T,
        "rw": a["L0_ffn_router_w"].T,
        "rb": a["L0_ffn_router_b"][None],
        "wq": np.stack([wqkv[:, :, 0].transpose(1, 2, 0).reshape(D, NH * HD), wqkv[:, :, 1].transpose(1, 2, 0).reshape(D, NH * HD),
                        wqkv[:, :, 2].transpose(1, 0, 2).reshape(D, NH * HD)], 1),
        "wout": a["L1_attn_W_out"].reshape(NH * HD, D),
        "gw": np.stack([a["L1_ffn_" + n].T for n in ("wf", "uf", "wi", "ui", "wc", "uc", "wo", "uo")], 1),
        "gbias": np.stack([a["L1_ffn_" + n] for n in ("bf", "bi", "bc", "bo", "in_c")], 1),
        "mask": np.stack([np.triu(np.full((P, P), -1e10, np.float32), 1), np.tril(np.full((P, P), -1e10, np.float32), -1)], 1),
        "ident": np.eye(P, dtype=np.float32),
        "ones": np.ones((P, P), np.float32),
        "rank": np.arange(NR, 0, -1, dtype=np.float32)[None],
    }


def kernel(**inputs):
    import concourse.bacc as _bacc
    from concourse.bass_utils import run_bass_kernel_spmd as _run

    nc = _bacc.Bacc("TRN2", target_bir_lowering=False, num_devices=1)
    arrays, aps = {}, {}
    for name, a in host_layout(inputs).items():
        a = np.ascontiguousarray(a)
        arrays[f"in_{name}"] = a
        aps[name] = nc.dram_tensor(f"in_{name}", a.shape, mybir.dt.from_np(a.dtype), kind="ExternalInput").ap()
    out = nc.dram_tensor("out_0", (NB, S, D), F32, kind="ExternalOutput").ap()
    build(nc, aps, out)
    r = _run(nc, [arrays], core_ids=[0])
    return r.results[0]["out_0"]
```
